# Optimizing a Trainium2 kernel written in Bass

```python
import numpy as np
import jax
import jax.numpy as jnp

def _softmax(x, axis=-1):
    return jax.nn.softmax(x, axis=axis)

def _gelu(x):
    return jax.nn.gelu(x, approximate=True)

def _silu(x):
    return jax.nn.silu(x)

def _sigmoid(x):
    return jax.nn.sigmoid(x)

def _layernorm(x, axis=-1, eps=1e-05):
    m = jnp.mean(x, axis=axis, keepdims=True)
    v = jnp.var(x, axis=axis, keepdims=True)
    return (x - m) / jnp.sqrt(v + eps)

def _scatter_add(tgt, idx, src, axis=0):
    return tgt.at[idx].add(src)

def _segment_sum(src, seg, n):
    return jax.ops.segment_sum(src, seg, n)
kernel_name = 'mk_xattn_ffn_d2_seqx_r4_72fc23'

def setup_inputs(seed: int=0):
    np.random.seed(seed)
    _w = jnp.asarray

    def _rec_inputs():
        import jax
        import jax.numpy as jnp
        _rk = jax.random.key(seed)
        x = 7.22e-05 + 1 * jax.random.normal(jax.random.fold_in(_rk, 1), (4, 512, 256), jnp.float32)
        _lenS = 512 - jax.random.randint(jax.random.fold_in(_rk, 7), (4,), 0, max(1, 512 // 4) + 1, jnp.int32)
        _lenS2 = 512 - jax.random.randint(jax.random.fold_in(_rk, 8), (4,), 0, max(1, 512 // 4) + 1, jnp.int32)
        _ctx_1024P = jax.random.normal(jax.random.fold_in(_rk, 11), (4, 16, 256), jnp.float32)
        _ctx_1024c = jax.random.dirichlet(jax.random.fold_in(_rk, 511), 0.3 * jnp.ones((16,), jnp.float32), (4, 512))
        _ctx_1024t = jnp.einsum('bsk,bkd->bsd', _ctx_1024c, _ctx_1024P)
        _ctx_1024t = _ctx_1024t * jax.lax.rsqrt(jnp.mean(jnp.square(_ctx_1024t)) + 1e-12) * 0.953939
        ctx_1024 = 4.13588e-05 + 0.999923 * (_ctx_1024t + 0.3 * jax.random.normal(jax.random.fold_in(_rk, 611), (4, 512, 256), jnp.float32))
        return (x, ctx_1024)
    x, ctx_1024 = _rec_inputs()

    def _L0_xattn_setup():
        import jax, jax.numpy as jnp
        import numpy as np
        import math
        D_MODEL = 256
        N_HEADS = 16
        D_K = D_MODEL // N_HEADS
        B, L = (4, 512)

        def _heads(x):
            b, l, _ = x.shape
            return x.reshape(b, l, N_HEADS, D_K).transpose(0, 2, 1, 3)
        key = jax.random.key(seed)
        ks = jax.random.split(key, 11)
        s = 1.0 / math.sqrt(D_MODEL)
        inp = {'queries': jax.random.normal(ks[0], (B, L, D_MODEL), jnp.float32), 'keys': jax.random.normal(ks[1], (B, L, D_MODEL), jnp.float32), 'values': jax.random.normal(ks[2], (B, L, D_MODEL), jnp.float32), 'Wq': jax.random.normal(ks[3], (D_MODEL, D_MODEL), jnp.float32) * s, 'bq': jax.random.normal(ks[4], (D_MODEL,), jnp.float32) * s, 'Wk': jax.random.normal(ks[5], (D_MODEL, D_MODEL), jnp.float32) * s, 'bk': jax.random.normal(ks[6], (D_MODEL,), jnp.float32) * s, 'Wv': jax.random.normal(ks[7], (D_MODEL, D_MODEL), jnp.float32) * s, 'bv': jax.random.normal(ks[8], (D_MODEL,), jnp.float32) * s, 'Wo': jax.random.normal(ks[9], (D_MODEL, D_MODEL), jnp.float32) * s, 'bo': jax.random.normal(ks[10], (D_MODEL,), jnp.float32) * s}
        return inp
    _L0_xattn_all = _L0_xattn_setup()
    _L0_xattn_in = {k: v for k, v in _L0_xattn_all.items() if k in ('Wq', 'bq', 'Wk', 'bk', 'Wv', 'bv', 'Wo', 'bo')}
    del _L0_xattn_all

    def _L0_ffn_setup():
        import jax, jax.numpy as jnp
        import numpy as np
        B, T, H = (2, 512, 256)
        I = 1024
        HEADS = 4
        RET = 128
        NUM_EXPERTS = 1024
        NUM_KEYS = 64
        K = 8
        key = jax.random.key(seed)
        ks = jax.random.split(key, 7)
        return {'hidden_states': jax.random.normal(ks[0], (B, T, H), jnp.float32), 'W_up': jax.random.normal(ks[1], (I, H), jnp.float32) * 0.02, 'W_down': jax.random.normal(ks[2], (H, I), jnp.float32) * 0.02, 'W_q': jax.random.normal(ks[3], (HEADS * RET, H), jnp.float32) * 0.02, 'keys': jax.random.normal(ks[4], (HEADS, NUM_KEYS, 2, RET // 2), jnp.float32) * 0.02, 'down_embed': jax.random.normal(ks[5], (NUM_EXPERTS, H), jnp.float32) * 0.02, 'up_embed': jax.random.normal(ks[6], (NUM_EXPERTS, H), jnp.float32) * 0.02}
    _L0_ffn_all = _L0_ffn_setup()
    _L0_ffn_in = {k: v for k, v in _L0_ffn_all.items() if k in ('W_up', 'W_down', 'W_q', 'keys', 'down_embed', 'up_embed')}
    del _L0_ffn_all

    def _L1_xattn_setup():
        import jax, jax.numpy as jnp
        import numpy as np
        BETA = 256
        NUM_HEADS = 16
        NORM = (BETA // NUM_HEADS) ** (-0.5)
        key = jax.random.key(seed)
        ks = jax.random.split(key, 6)
        B, N = (4, 512)
        D_in_q = D_in_k = D_in_v = 256
        D_out_k = D_out_v = 256
        q = jax.random.normal(ks[0], (B, N, D_in_q), dtype=jnp.float32)
        k = jax.random.normal(ks[1], (B, N, D_in_k), dtype=jnp.float32)
        v = jax.random.normal(ks[2], (B, N, D_in_v), dtype=jnp.float32)
        Wq = jax.random.normal(ks[3], (D_out_k, D_in_q), dtype=jnp.float32) * D_in_q ** (-0.5)
        Wk = jax.random.normal(ks[4], (D_out_k, D_in_k), dtype=jnp.float32) * D_in_k ** (-0.5)
        Wv = jax.random.normal(ks[5], (D_out_v, D_in_v), dtype=jnp.float32) * D_in_v ** (-0.5)
        return {'q': q, 'k': k, 'v': v, 'Wq': Wq, 'Wk': Wk, 'Wv': Wv}
    _L1_xattn_all = _L1_xattn_setup()
    _L1_xattn_in = {k: v for k, v in _L1_xattn_all.items() if k in ('Wq', 'Wk', 'Wv')}
    del _L1_xattn_all

    def _L1_ffn_setup():
        import jax, jax.numpy as jnp
        import numpy as np
        E = 8
        K = 2
        C = 256
        F = 512
        EPS = 1e-05
        key = jax.random.key(seed)
        ks = jax.random.split(key, 6)
        x = jax.random.normal(ks[0], (2, 256, C), dtype=jnp.float32)
        ln_gamma = 1.0 + 0.02 * jax.random.normal(ks[1], (C,), dtype=jnp.float32)
        ln_beta = 0.02 * jax.random.normal(ks[2], (C,), dtype=jnp.float32)
        gate_w = jax.random.normal(ks[3], (E, C), dtype=jnp.float32) / np.sqrt(C)
        w1 = jax.random.normal(ks[4], (E, F, C), dtype=jnp.float32) / np.sqrt(C)
        w2 = jax.random.normal(ks[5], (E, C, F), dtype=jnp.float32) / np.sqrt(F)
        return {'x': x, 'ln_gamma': ln_gamma, 'ln_beta': ln_beta, 'gate_w': gate_w, 'w1': w1, 'w2': w2}
    _L1_ffn_all = _L1_ffn_setup()
    _L1_ffn_in = {k: v for k, v in _L1_ffn_all.items() if k in ('ln_gamma', 'ln_beta', 'gate_w', 'w1', 'w2')}
    del _L1_ffn_all
    return {'x': x, 'ctx_1024': ctx_1024, 'L0_xattn_Wq': _L0_xattn_in['Wq'], 'L0_xattn_bq': _L0_xattn_in['bq'], 'L0_xattn_Wk': _L0_xattn_in['Wk'], 'L0_xattn_bk': _L0_xattn_in['bk'], 'L0_xattn_Wv': _L0_xattn_in['Wv'], 'L0_xattn_bv': _L0_xattn_in['bv'], 'L0_xattn_Wo': _L0_xattn_in['Wo'], 'L0_xattn_bo': _L0_xattn_in['bo'], 'L0_ffn_W_up': _L0_ffn_in['W_up'], 'L0_ffn_W_down': _L0_ffn_in['W_down'], 'L0_ffn_W_q': _L0_ffn_in['W_q'], 'L0_ffn_keys': _L0_ffn_in['keys'], 'L0_ffn_down_embed': _L0_ffn_in['down_embed'], 'L0_ffn_up_embed': _L0_ffn_in['up_embed'], 'L1_xattn_Wq': _L1_xattn_in['Wq'], 'L1_xattn_Wk': _L1_xattn_in['Wk'], 'L1_xattn_Wv': _L1_xattn_in['Wv'], 'L1_ffn_ln_gamma': _L1_ffn_in['ln_gamma'], 'L1_ffn_ln_beta': _L1_ffn_in['ln_beta'], 'L1_ffn_gate_w': _L1_ffn_in['gate_w'], 'L1_ffn_w1': _L1_ffn_in['w1'], 'L1_ffn_w2': _L1_ffn_in['w2']}

def reference(x, ctx_1024, L0_xattn_Wq, L0_xattn_bq, L0_xattn_Wk, L0_xattn_bk, L0_xattn_Wv, L0_xattn_bv, L0_xattn_Wo, L0_xattn_bo, L0_ffn_W_up, L0_ffn_W_down, L0_ffn_W_q, L0_ffn_keys, L0_ffn_down_embed, L0_ffn_up_embed, L1_xattn_Wq, L1_xattn_Wk, L1_xattn_Wv, L1_ffn_ln_gamma, L1_ffn_ln_beta, L1_ffn_gate_w, L1_ffn_w1, L1_ffn_w2):
    import jax
    import jax.numpy as jnp

    def _L0_xattn_ref(queries, keys, values, Wq, bq, Wk, bk, Wv, bv, Wo, bo):
        import jax, jax.numpy as jnp
        import numpy as np
        import math
        D_MODEL = 256
        N_HEADS = 16
        D_K = D_MODEL // N_HEADS
        B, L = (4, 512)

        def _heads(x):
            b, l, _ = x.shape
            return x.reshape(b, l, N_HEADS, D_K).transpose(0, 2, 1, 3)
        Q = _heads(queries @ Wq.T + bq)
        K = _heads(keys @ Wk.T + bk)
        V = _heads(values @ Wv.T + bv)
        scores = jnp.einsum('bhqd,bhkd->bhqk', Q, K) / math.sqrt(D_K)
        t = jnp.arange(L, dtype=scores.dtype)
        time_bias = -0.1 * jnp.abs(t[None, :] - t[:, None])
        attn = jax.nn.softmax(scores + time_bias[None, None], axis=-1)
        out = jnp.einsum('bhqk,bhkd->bhqd', attn, V)
        out = out.transpose(0, 2, 1, 3).reshape(queries.shape[0], L, D_MODEL)
        return out @ Wo.T + bo

    def _L0_ffn_ref(hidden_states, W_up, W_down, W_q, keys, down_embed, up_embed):
        import jax, jax.numpy as jnp
        import numpy as np
        B, T, H = (2, 512, 256)
        I = 1024
        HEADS = 4
        RET = 128
        NUM_EXPERTS = 1024
        NUM_KEYS = 64
        K = 8
        b, t, hd = hidden_states.shape
        h, nk, _, n = keys.shape
        q = jnp.einsum('btd,ed->bte', hidden_states, W_q)
        q = q.reshape(b, t, 2, h, n).transpose(2, 0, 1, 3, 4)
        sim = jnp.einsum('pbthn,hkpn->pbthk', q, keys)
        scores_xy, idx_xy = jax.lax.top_k(sim, K)
        sx, sy = (scores_xy[0], scores_xy[1])
        ix, iy = (idx_xy[0], idx_xy[1])
        all_scores = (sx[..., :, None] + sy[..., None, :]).reshape(b, t, h, K * K)
        all_idx = (ix[..., :, None] * nk + iy[..., None, :]).reshape(b, t, h, K * K)
        scores, pk = jax.lax.top_k(all_scores, K)
        indices = jnp.take_along_axis(all_idx, pk, axis=-1)
        de = down_embed[indices]
        ue = up_embed[indices]
        w = jax.nn.silu(jnp.einsum('btd,bthkd->bthk', hidden_states, de) * jax.nn.softmax(scores, axis=-1))
        experts_states = jnp.einsum('bthk,bthkd->btd', w, ue)
        dense = jnp.einsum('bti,di->btd', jax.nn.silu(jnp.einsum('btd,id->bti', hidden_states, W_up)), W_down)
        return dense + experts_states

    def _L1_xattn_ref(q, k, v, Wq, Wk, Wv):
        import jax, jax.numpy as jnp
        import numpy as np
        BETA = 256
        NUM_HEADS = 16
        NORM = (BETA // NUM_HEADS) ** (-0.5)
        qp = jax.nn.relu(jnp.einsum('bnd,od->bno', q, Wq))
        kp = jax.nn.relu(jnp.einsum('bnd,od->bno', k, Wk))
        vp = jax.nn.relu(jnp.einsum('bnd,od->bno', v, Wv))
        B, N, D = qp.shape
        dh = D // NUM_HEADS
        qh = qp.reshape(B, N, NUM_HEADS, dh)
        kh = kp.reshape(B, N, NUM_HEADS, dh)
        vh = vp.reshape(B, N, NUM_HEADS, vp.shape[-1] // NUM_HEADS)
        E = NORM * jnp.einsum('bqhd,bkhd->bhqk', qh, kh)
        A = jax.nn.softmax(E, axis=-1)
        out = jnp.einsum('bhqk,bkhd->bqhd', A, vh)
        return out.reshape(B, N, -1)

    def _L1_ffn_ref(x, ln_gamma, ln_beta, gate_w, w1, w2):
        import jax, jax.numpy as jnp
        import numpy as np
        E = 8
        K = 2
        C = 256
        F = 512
        EPS = 1e-05
        B, T, Cc = x.shape
        xf = x.reshape(-1, Cc)
        mu = jnp.mean(xf, axis=-1, keepdims=True)
        var = jnp.var(xf, axis=-1, keepdims=True)
        rn = (xf - mu) * jax.lax.rsqrt(var + EPS) * ln_gamma + ln_beta
        logits = rn @ gate_w.T
        probs = jax.nn.softmax(logits, axis=-1)
        rw, sel = jax.lax.top_k(probs, K)
        comb = jnp.sum(jax.nn.one_hot(sel, E, dtype=xf.dtype) * rw[..., None], axis=1)
        h = jax.nn.gelu(jnp.einsum('nc,efc->enf', xf, w1), approximate=False)
        y = jnp.einsum('enf,ecf->enc', h, w2)
        out = jnp.einsum('enc,ne->nc', y, comb)
        return out.reshape(B, T, Cc)
    x = x + _L0_xattn_ref(_layernorm(x, axis=-1), ctx_1024, ctx_1024, L0_xattn_Wq, L0_xattn_bq, L0_xattn_Wk, L0_xattn_bk, L0_xattn_Wv, L0_xattn_bv, L0_xattn_Wo, L0_xattn_bo)
    x = x + _L0_ffn_ref(_layernorm(x, axis=-1), L0_ffn_W_up, L0_ffn_W_down, L0_ffn_W_q, L0_ffn_keys, L0_ffn_down_embed, L0_ffn_up_embed)
    x = x + _L1_xattn_ref(_layernorm(x, axis=-1), ctx_1024, ctx_1024, L1_xattn_Wq, L1_xattn_Wk, L1_xattn_Wv)
    x = x + _L1_ffn_ref(_layernorm(x, axis=-1), L1_ffn_ln_gamma, L1_ffn_ln_beta, L1_ffn_gate_w, L1_ffn_w1, L1_ffn_w2)
    return x

_drawn_inputs = setup_inputs


def setup_inputs(seed=0):
    import zlib

    import numpy as np

    out = dict(_drawn_inputs(seed))
    spreads = {}
    factors = {'L0_xattn_bq': 3.164,
     'L0_xattn_bk': 200.0,
     'L0_ffn_W_q': 8.0,
     'L0_ffn_keys': 8.0,
     'L0_ffn_down_embed': 4.575,
     'L0_ffn_up_embed': 5.056,
     'L1_ffn_ln_gamma': 29.244,
     'L1_ffn_ln_beta': 25.209}
    for name, (base, spread) in spreads.items():
        noise = np.random.default_rng([zlib.crc32(name.encode()), seed]).standard_normal(out[name].shape)
        drawn = base * np.exp(spread * noise) if base else spread * noise
        out[name] = jnp.asarray(drawn.astype(out[name].dtype))
    for name, factor in factors.items():
        out[name] = (out[name] * factor).astype(out[name].dtype)
    return out
```

```python
from contextlib import ExitStack

import numpy as np

import concourse.bass as bass
from concourse import mybir

ALU = mybir.AluOpType
ACT = mybir.ActivationFunctionType
AX = mybir.AxisListType.X
F32 = mybir.dt.float32
F32R = mybir.dt.float32r
F16 = mybir.dt.float16
U32 = mybir.dt.uint32

P = 128
B, T, D = 4, 512, 256
TT, KC = T // P, D // P
H, DH = 16, 16
HG = 4
NG = H // HG
NU = NG * TT
SCALE = DH ** -0.5
SLOTS = 3
PR = 2 * DH
BROW = 3 * PR
MROW = BROW + 16
BIAS = 0.1
LEAD = 6

FF = 1024
FC = FF // P
NE = 1024
EC = NE // P
RH, NK, RD, TOPK = 4, 64, 64, 8
NX = NE // NK
TROWS = 96
R_LOGIT, R_THR = NK + NX, NK + NX + 1
DELTA = 2.0 ** -22

ME, MF = 8, 512
MC = MF // P
EPS = 1e-5


def shape_constants():
    k = np.arange(T)
    cut = lambda v: (np.asarray(v, np.float32).view(np.uint32) & np.uint32(0xFFFFF000)).view(np.float32)
    kb, qb = np.zeros((16, T), np.float32), np.zeros((16, T), np.float32)
    for c in range(TT):
        here = (k // P == c)
        line = np.where(here, -np.float32(BIAS), 0).astype(np.float32)
        slope = np.where(here, np.float32(BIAS) * (k - P * c), 0).astype(np.float32)
        for r, v in ((0, line), (2, slope)):
            kb[4 * c + r], kb[4 * c + r + 1] = cut(v), v - cut(v)
        qb[4 * c] = qb[4 * c + 1] = np.where(here, 0, np.abs(k - P * c))
        qb[4 * c + 2] = qb[4 * c + 3] = np.sign(k // P - c)
    i = np.arange(P)
    sel = np.zeros((TROWS, EC, 2, P), np.float32)
    for c in range(EC):
        sel[i % NK, c, :, i] = 1
        sel[NK + 2 * c + i // NK, c, :, i] = 1
        sel[R_LOGIT, c, 0, i] = 1
        sel[R_THR, c, 1, i] = 1
    return {
        "c_ident": np.eye(P, dtype=np.float32),
        "c_neg": -np.float32(BIAS) * np.eye(P, dtype=np.float32),
        "c_dist": np.abs(i[:, None] - i[None, :]).astype(np.float32),
        "c_kb": kb, "c_qb": qb,
        "c_par": np.stack([(i // DH) % 2 == 0, (i // DH) % 2 == 1], 1).astype(np.float32),
        "c_sel": sel.reshape(TROWS, -1),
    }


class Own:

    def __init__(self, eng, sem, n, b):
        self.eng, self.sem, self.n, self.b, self.k = eng, sem, n, b, 0

    def __call__(self, ins):
        ins.then_inc(self.sem, 1)
        self.k += 1

    def wait(self, alone=False):
        self.eng.wait_ge(self.sem, self.b * self.n + self.k)
        if alone:
            self.eng.nop(nofuse=True)

    def close(self):
        assert self.k == self.n, (self.k, self.n)


def build(nc, a, out):
    ctx = ExitStack()
    with ctx:
        sb = lambda name, shape, dt=F32: ctx.enter_context(nc.sbuf_tensor(name, shape, dt))
        sem = lambda name: ctx.enter_context(nc.semaphore(name))

        wq = [sb(f"wq{l}", [P, KC, D]) for l in range(2)]
        wk = [sb(f"wk{l}", [P, KC, D]) for l in range(2)]
        wv = [sb(f"wv{l}", [P, KC, D]) for l in range(2)]
        wo = sb("wo", [P, KC, D])
        wret = sb("wret", [P, KC, RH * 2 * NK])
        wdown_e = sb("wdown_e", [P, KC, NE])
        wup_e = sb("wup_e", [P, EC, D])
        wff1 = sb("wff1", [P, KC, FF])
        wff2 = sb("wff2", [P, FC, D])
        gw = sb("gw", [P, KC, ME])
        gcol = sb("gcol", [P, 2 * KC])
        gbc = sb("gbc", [P, 2, ME])
        bqk = sb("bqk", [P, 2, KC])
        bv_bc = sb("bv_bc", [P, D])
        bo_bc = sb("bo_bc", [P, D])
        last_up = sb("last_up", [P, D])
        ident = sb("ident", [P, P])
        ones = sb("ones", [P, P])
        neg16 = sb("neg16", [P, 2, P], F16)
        dist16 = sb("dist16", [P, P], F16)
        sel = sb("sel", [TROWS, EC, 2, P], F32R)
        qb_c = sb("qb_c", [16, 2, T], F32R)
        x_in = sb("x_in", [P, TT, D])
        ctx_in = sb("ctx_in", [P, TT, D])
        x_tok = sb("x_tok", [P, TT, D])
        xn = sb("xn", [P, TT, D])
        xnT = sb("xnT", [P, KC, T])
        ctxT = sb("ctxT", [P, KC, T])
        v_aug = sb("v_aug", [P, TT, H, 32])
        par = sb("par", [P, 2])
        qs = sb("qs", [P, 2, KC, 2, T], F32R)
        ks = sb("ks", [P, 2, KC, T], F32R)
        pt = sb("pt", [P, 8, T])
        moe_w = sb("moe_w", [P, 2, 2 * MC * D])
        g_parts = sb("g_parts", [P, 4, T], F32R)
        oT = sb("oT", [P, T])
        stack_q = [sb(f"stack_q{s}", [P, HG, T], F32R) for s in range(SLOTS)]
        stack_k = [sb(f"stack_k{s}", [MROW + 1, HG // 2, T], F32R) for s in range(SLOTS)]
        negmax = sb("negmax", [P, 2, HG * TT])
        m_sb = sb("m_sb", [HG * TT, 2, P], F32R)
        rec = sb("rec", [P, TT, HG])
        st6 = sb("st6", [P, TT, 6])
        mv = sb("mv", [P, TT, 2])
        ve = sb("ve", [P, TT])
        sd = sb("sd", [P, TT])
        rstd = sb("rstd", [P, TT])
        ffh = sb("ffh", [P, 2, T])
        sx8 = sb("sx8", [P, TT * RH, 8])
        sy8 = sb("sy8", [P, TT * RH, 8])
        ix8 = sb("ix8", [P, TT * RH, 8], U32)
        ixg = sb("ixg", [P, TT * RH, 8])
        v8 = sb("v8", [P, TT * RH, 8])
        e8 = sb("e8", [P, TT * RH, 8])
        zz = sb("zz", [P, TT * RH])
        lnz = sb("lnz", [P, TT * RH])
        mag = sb("mag", [P, 2, TT * RH])
        hdc = sb("hdc", [P, TT])
        wc = sb("wc", [P, TT])
        c64 = sb("c64", [P, TT * RH, 64])
        lg = sb("lg", [P, TT, ME])
        lg2 = sb("lg2", [P, TT, ME])
        mx8 = sb("mx8", [P, TT, 8])
        ee = sb("ee", [P, TT, ME])
        gz = sb("gz", [P, TT])
        comb = sb("comb", [P, TT, ME])
        simcat = moe_w[:, 0, :].rearrange("p (t h c) -> p t h c", t=TT, h=RH)
        s64 = moe_w[:, 1, 0:1024].rearrange("p (a c) -> p a c", c=64)
        e64 = moe_w[:, 1, 1024:2048].rearrange("p (a c) -> p a c", c=64)
        tr = qs[0:TROWS].rearrange("p i k h t -> p (i k h) t")
        pexp = [pt[:, i, :] for i in range(3)]
        pv_b = [pt[:, 3 + i, :] for i in range(3)]
        pth = [pt[:, 6 + i, :] for i in range(2)]
        qf, kf = pt[:, 0:2, :], pt[:, 2:4, :]
        two = lambda buf: buf[:].rearrange("p (a b) d -> p a (b d)", a=2)
        hdT, acc, wt = two(x_in), two(ctx_in), two(xn)
        flat = lambda buf: buf[:].rearrange("p a b -> p (a b)")
        parts = lambda v: v.rearrange("p (i t) -> p i t", i=2)
        qs_flat = qs[:].rearrange("p i k h t -> p (i k h t)")
        xs = ks
        w1s = [v.rearrange("p (i k f) -> p i k f", i=2, k=KC) for v in (qs_flat[:, 0:2 * KC * MF], flat(stack_q[0]))]
        w2s = [v.rearrange("p (i k f) -> p i k f", i=2, k=MC) for v in (qs_flat[:, 2 * KC * MF:], flat(stack_q[1]))]
        gs = [parts(flat(buf)[:, 2 * T * f:2 * T * (f + 1)]) for buf in (stack_q[2], g_parts) for f in range(2)]
        g_raw = two(xn)
        kb_c = g_parts[0:16, 0, :]
        w1b = [moe_w[:, s, 0:1024].rearrange("p (k f) -> p k f", k=KC) for s in range(2)]
        w2b = [moe_w[:, s, 1024:2048].rearrange("p (k f) -> p k f", k=MC) for s in range(2)]
        st_sel = pt[0:TROWS, 0:4, :].rearrange("p a b -> p (a b)")
        st_kb, st_qb = pt[0:16, 4, :], pt[0:16, 5, :]
        st_neg, st_dist = pt[:, 6, 0:P], pt[:, 6, P:2 * P]
        st_negh = pt[:, 6, 2 * P:3 * P]
        st_wq = moe_w[0:RD, 0, :].rearrange("p (a d) -> p a d", d=D)
        st_keys = moe_w[0:RD, 1, 0:RH * 2 * NK]

        ps = ctx.enter_context(nc.psum_tensor("ps", [P, 8, 512], F32))

        s_w = sem("weights_in"); s_ci = sem("consts_in")
        s_conv = sem("consts_ready"); s_ms = sem("memsets_done"); s_wret_ps = sem("wret_psum")
        s_wret = sem("wret_ready"); s_gi = sem("gate_psum"); s_kbin = sem("bias_rows_in")
        s_x = sem("x_in"); s_ctx = sem("ctx_in")
        s_lnv = sem("ln_var"); s_lnd = sem("ln_sd")
        s_ln = sem("ln_out")
        s_tr = sem("transposes_psum")
        s_tra = sem("transposed_act"); s_trd = sem("transposed_dve")
        s_qk = sem("qk_psum"); s_qkf = sem("qk_float")
        s_split = sem("qk_split")
        s_v = sem("v_psum"); s_va = sem("v_ready")
        s_stk = [[sem(f"stack_in{s}_{i}") for i in range(HG // 2)] for s in range(SLOTS)]
        slot_turn = lambda n: (len(range(n % SLOTS, 2 * NG, SLOTS)), n // SLOTS)
        s_s = sem("scores_psum"); s_red = sem("max_reduced")
        s_mt = sem("max_turned"); s_mc = sem("max_copied")
        s_mr = [sem(f"max_rows_in{i}") for i in range(2)]
        s_st = sem("scoresT_psum"); s_e = sem("probs_ready")
        s_pv = sem("pv_psum"); s_oT = sem("o_copied")
        s_ot = sem("o_turned"); s_on = sem("o_normed")
        s_wo = sem("wo_psum"); s_x1 = sem("x1_added")
        s_xb = sem("x_plus_bo")
        s_sim = sem("sim_psum"); s_simc = sem("sim_copied")
        s_hc = sem("hd_last_psum"); s_hcc = sem("hd_last_copied")
        s_f = sem("ff_psum"); s_fs = sem("ff_silu"); s_fd = sem("ff_down")
        s_d8 = sem("top8_shifted"); s_e8 = sem("top8_exp")
        s_z8 = sem("top8_sum"); s_l8 = sem("top8_log")
        s_a64 = sem("pairs_shifted"); s_x64 = sem("pairs_exp")
        s_c64 = sem("pairs_masked"); s_wc = sem("clamped_weight")
        s_row = sem("sim_rows_ready"); s_tt = sem("sim_turned")
        s_th = sem("sim_hi"); s_tl = sem("sim_lo")
        s_hd = sem("hd_psum"); s_hdc = sem("hd_copied")
        s_l = sem("logit_psum"); s_m = sem("mask_psum")
        s_pe = sem("p_exp"); s_pm = sem("p_masked")
        s_u = sem("u_ready"); s_t = sem("tanh_ready"); s_g = sem("gated")
        s_acc = sem("expert_weights"); s_yu = sem("y_up")
        s_gp = sem("gate_logits_psum"); s_gm = sem("gate_shifted"); s_ge = sem("gate_exp")
        s_mw = [sem(f"moe_w1_in{i}") for i in range(2)]
        s_mv = [sem(f"moe_w2_in{i}") for i in range(2)]
        s_w1h = sem("moe_w1_hi"); s_w1s = sem("moe_w1_split")
        s_w2h = sem("moe_w2_hi"); s_w2s = sem("moe_w2_split")
        s_xh = sem("moe_x_hi"); s_xl = sem("moe_x_split")
        s_mu = sem("moe_up_psum"); s_mg = sem("moe_gelu")
        s_gl = sem("moe_gelu_split"); s_mf = sem("moe_tile_used")
        s_md = sem("moe_down_psum"); s_ma = sem("moe_added")
        s_o = sem("out_stored")
        s_own = sem("dve_own"); s_owni = sem("dve_own_init")

        NW = 25
        NCI = 7
        STK = (16 * 7, 16 * 6)

        block = ctx.enter_context(nc.Block())

        @block.sync
        def _(sp):
            for dst, src in (
                (st_kb, a["c_kb"]), (st_qb, a["c_qb"]), (st_neg, a["c_neg"]), (st_dist, a["c_dist"]),
                (ident[:], a["c_ident"]), (st_sel, a["c_sel"]), (par[:], a["c_par"]),
            ):
                sp.dma_start(dst, src).then_inc(s_ci, 16)
            kcut = lambda w: w.rearrange("(k p) n -> p k n", p=P)
            row = lambda v: v.rearrange("(a n) -> a n", a=1).broadcast_to([P, D])
            n = 0
            for dst, src in (
                (wq[0][:], kcut(a["wq0"])), (wk[0][:], kcut(a["wk0"])), (wv[0][:], kcut(a["wv0"])),
                (bqk[:, 0, :], a["bq"]), (bqk[:, 1, :], a["bk"]),
                (bv_bc[:], row(a["bv"])), (bo_bc[:], row(a["bo"])), (wo[:], kcut(a["wo0"])),
                (st_wq, a["w_ret"].rearrange("(a n) d -> n a d", n=RD)), (st_keys, a["keys"].rearrange("n h p k -> n (h p k)")),
                (wdown_e[:], kcut(a["down_e"])), (wup_e[:], kcut(a["up_e"])), (wff1[:], kcut(a["ff1"])), (wff2[:], kcut(a["ff2"])),
                (last_up[:], a["up_e"][NE - 1:NE, :].broadcast_to([P, D])),
                (wq[1][:], kcut(a["wq1"])), (wk[1][:], kcut(a["wk1"])), (wv[1][:], kcut(a["wv1"])),
                (gw[:], kcut(a["gate"])), (gcol[:, 0:KC], a["gamma"]),
                (gcol[:, KC:2 * KC], a["beta"]),
            ):
                sp.dma_start(dst, src).then_inc(s_w, 16)
                n += 1
            sp.wait_ge(s_conv, 4)
            sp.wait_ge(s_ms, 3 + SLOTS)
            for s in range(SLOTS):
                sp.dma_start(stack_k[s][BROW:BROW + 16, :, :].bitcast(F32),
                             kb_c.bitcast(F32).unsqueeze(1).broadcast_to([16, HG // 2, T])).then_inc(s_kbin, 16)
            assert n == 21

            with sp.Fori(0, B) as b:
                def wait(s, value):
                    sp.wait_ge(s, value)
                    sp.nop(nofuse=True)

                if True:
                    sp.dma_start(x_in[:], a["x"][b].rearrange("(t p) d -> p t d", p=P)).then_inc(s_x, 16)
                    sp.dma_start(ctx_in[:], a["ctx"][b].rearrange("(t p) d -> p t d", p=P)).then_inc(s_ctx, 16)

                def load_stack(L, g):
                    n = NG * L + g
                    s = n % SLOTS
                    if n >= SLOTS:
                        wait(s_st, b * 64 + 8 * (n - SLOTS) + 8)
                    if g % 2 == 0:
                        wait(s_split, b * 4 + 2 * L + g // 2 + 1)
                    sp.dma_start(stack_q[s][BROW:BROW + 16, :, :].bitcast(F32),
                                 qb_c[:, L, :].bitcast(F32).unsqueeze(1).broadcast_to([16, HG, T])).then_inc(s_stk[s][0], 16)
                    for pair in range(HG // 2):
                        r, m = PR * (2 * (g % 2) + pair), g // 2
                        for blk, qi, ki in ((0, 0, 0), (1, 1, 0), (2, 0, 1)):
                            rows = slice(PR * blk, PR * (blk + 1))
                            sp.dma_start(stack_q[s][rows, 2 * pair:2 * pair + 2, :].bitcast(F32), qs[r:r + PR, qi, m, :, :].bitcast(F32)).then_inc(s_stk[s][pair], 16)
                            sp.dma_start(stack_k[s][rows, pair, :].bitcast(F32), ks[r:r + PR, ki, m, :].bitcast(F32)).then_inc(s_stk[s][pair], 16)

                def load_max(L, g):
                    n = NG * L + g
                    wait(s_mc, b * 8 + n + 1)
                    sp.dma_start(stack_q[n % SLOTS][MROW:MROW + 1, :, :].bitcast(F32),
                                 m_sb[:, n % 2, :].bitcast(F32)).then_inc(s_mr[n % 2], 16)

                for L in range(2):
                    for what, g in ((load_stack, 0), (load_stack, 1), (load_max, 0), (load_stack, 2), (load_max, 1),
                                    (load_stack, 3), (load_max, 2), (load_max, 3)):
                        what(L, g)
                for e in range(ME):
                    s = e % 2
                    if e >= 2:
                        wait(s_w1s, b * ME + e - 1)
                    sp.dma_start(w1b[s], a["w1"][e].rearrange("(k p) f -> p k f", p=P)).then_inc(s_mw[s], 16)
                    if e >= 2:
                        wait(s_w2s, b * ME + e - 1)
                    sp.dma_start(w2b[s], a["w2"][e].rearrange("(k p) f -> p k f", p=P)).then_inc(s_mv[s], 16)
                wait(s_yu, b * 8 + 8)

        @block.gpsimd
        def _(pool):
            fills = [(ones[:], 1.0), (v_aug[:], 0.0), (v_aug[:, :, :, DH:DH + 1], 1.0)]
            for s in range(SLOTS):
                fills += [(stack_k[s][96:MROW + 1, :, :].bitcast(F32), 1.0)]
            for i, (dst, value) in enumerate(fills):
                if i:
                    pool.wait_ge(s_ms, i)
                pool.memset(dst, value).then_inc(s_ms, 1)
            pool.wait_ge(s_ms, 3 + SLOTS)
            with pool.Fori(0, B) as b:
                pool.wait_ge(s_w, 16 * 21)
                pool.wait_ge(s_ln, b * 4 + 1)
                pool.tensor_tensor(x_in[:], x_in[:], bo_bc[:].unsqueeze(1).broadcast_to([P, TT, D]), ALU.add).then_inc(s_xb, 1)
                for q in range(EC * RH):
                    c = q // RH
                    pool.wait_ge(s_pm, b * 32 + q + 1)
                    if q % RH == 0:
                        pool.wait_ge(s_hdc, b * 8 + c + 1)
                    if q >= 3:
                        pool.wait_ge(s_g, b * 32 + q - 2)
                    pool.tensor_tensor(pv_b[q % 3], pexp[q % 3], hdT[:, c % 2, :], ALU.mult).then_inc(s_u, 1)
                pool.wait_ge(s_u, b * 32 + 32)
                def split_w1(e):
                    i = e % 2
                    if e == 0:
                        pool.wait_ge(s_mw[i], b * 64 + 16)
                        pool.wait_ge(s_red, b * 128 + 128)
                        pool.nop(nofuse=True)
                        pool.tensor_copy(w1s[i][:, 0], w1b[i]).then_inc(s_w1h, 1)
                    elif e >= 2:
                        pool.wait_ge(s_w2s, b * ME + e - 1)
                    else:
                        pool.wait_ge(s_w1s, b * ME + 1)
                    pool.wait_ge(s_w1h, b * ME + e + 1)
                    pool.tensor_tensor(w1s[i][:, 1], w1b[i], w1s[i][:, 0].bitcast(F32), ALU.subtract).then_inc(s_w1s, 1)

                split_w1(0)
                for e in range(ME):
                    if e + 1 < ME:
                        split_w1(e + 1)
                        pool.wait_ge(s_w1s, b * ME + e + 2)
                    else:
                        pool.wait_ge(s_w2s, b * ME + e)
                    pool.wait_ge(s_w2h, b * ME + e + 1)
                    pool.tensor_tensor(w2s[e % 2][:, 1], w2b[e % 2], w2s[e % 2][:, 0].bitcast(F32), ALU.subtract).then_inc(s_w2s, 1)
                pool.wait_ge(s_w2s, b * ME + ME)
                pool.wait_ge(s_ma, b * 32 + 32)
                pool.dma_start(out[b].rearrange("(t p) d -> p t d", p=P), x_tok[:]).then_inc(s_o, 16)
                pool.wait_ge(s_o, b * 16 + 16)

        @block.scalar
        def _(act):
            with act.Fori(0, B) as b:
                def sqrt(i):
                    act.wait_ge(s_lnv, b * 5 + i + 1)
                    act.activation(sd[:], ve[:], ACT.Sqrt).then_inc(s_lnd, 1)

                def turned(i, dst, bank):
                    act.wait_ge(s_tr, b * 6 + i + 1)
                    act.copy(dst, ps[:, bank, :]).then_inc(s_tra, 1)

                def to_float(L, which):
                    for m in range(KC):
                        act.wait_ge(s_qk, b * 8 + 4 * L + 2 * (1 - which) + m + 1)
                        dst = (qf, kf)[which][:, m, :]
                        scale = (SCALE, 1.0)[which]
                        if L == 0:
                            act.activation(dst, ps[:, 2 * which + m, :], ACT.Identity, bias=bqk[:, which, m:m + 1], scale=scale).then_inc(s_qkf, 1)
                        else:
                            act.activation(dst, ps[:, 2 * which + m, :], ACT.Relu, scale=scale).then_inc(s_qkf, 1)

                def attend(L):
                    for u in range(-LEAD, NU + 1):
                        v = u + LEAD
                        if 0 <= u < NU:
                            if u >= 2:
                                act.wait_ge(s_pv, b * 32 + NU * L + u - 1)
                            for half in range(2):
                                act.wait_ge(s_st, b * 64 + 2 * (NU * L + u) + half + 1)
                                act.activation(pt[:, 4 * (u % 2) + 2 * half:4 * (u % 2) + 2 * half + 2, :],
                                               ps[:, 2 + 2 * half:4 + 2 * half, :], ACT.Exp).then_inc(s_e, 1)
                        if v > 0 and v % 4 == 0 and v <= NU:
                            n = NG * L + v // 4 - 1
                            act.wait_ge(s_mt, b * 8 + n + 1)
                            if n >= 2:
                                act.wait_ge(s_mr[n % 2], b * 64 + 16 * (n // 2))
                            act.copy(m_sb[:, n % 2, :], ps[0:HG * TT, 7, 0:P]).then_inc(s_mc, 1)
                        if u > 0 and u % 4 == 0:
                            n = NG * L + u // 4 - 1
                            act.wait_ge(s_pv, b * 32 + 4 * n + 4)
                            if n >= 1:
                                act.wait_ge(s_ot, b * 8 + n)
                            act.copy(oT[:], ps[:, 6, :]).then_inc(s_oT, 1)

                turned(0, ctxT[:, 0, :], 2)
                sqrt(0)
                act.wait_ge(s_conv, 5)
                to_float(0, 1)
                turned(1, xnT[:, 0, :], 0)
                to_float(0, 0)
                attend(0)
                turned(2, xnT[:, 0, :], 0)
                sqrt(1)
                turned(3, xnT[:, 0, :], 0)
                for t in range(TT):
                    act.wait_ge(s_sim, b * 4 + t + 1)
                    act.copy(simcat[:, t, :, :].rearrange("p h c -> p (h c)"), ps[:, 2 + t, :]).then_inc(s_simc, 1)
                act.wait_ge(s_hc, b + 1)
                act.copy(hdc[:], ps[:, 6, 0:TT]).then_inc(s_hcc, 1)
                for f in range(FC):
                    act.wait_ge(s_f, b * 8 + f + 1)
                    if f >= 2:
                        act.wait_ge(s_fd, b * 8 + f - 1)
                    act.activation(ffh[:, f % 2, :], ps[:, f % 2, :], ACT.Silu).then_inc(s_fs, 1)
                act.wait_ge(s_d8, b + 1)
                act.activation(e8[:], v8[:], ACT.Exp).then_inc(s_e8, 1)
                act.wait_ge(s_z8, b + 1)
                act.activation(lnz[:], zz[:], ACT.Ln).then_inc(s_l8, 1)
                act.wait_ge(s_a64, b + 1)
                act.activation(e64, e64, ACT.Exp).then_inc(s_x64, 1)
                for h in range(RH):
                    act.wait_ge(s_tt, b * 4 + h + 1)
                    act.copy(tr[:, 2 * h, :], ps[0:TROWS, 2 + h, :]).then_inc(s_th, 1)
                for q in range(EC * RH + 2):
                    c, h = divmod(q, RH)
                    if q < EC * RH:
                        if h == 0:
                            act.wait_ge(s_hd, b * 8 + c + 1)
                            if c >= 2:
                                act.wait_ge(s_u, b * 32 + RH * (c - 1))
                            act.activation(hdT[:, c % 2, :], ps[:, c % 2, :], ACT.Copy, scale=0.5).then_inc(s_hdc, 1)
                        act.wait_ge(s_l, b * 32 + q + 1)
                        if q >= 3:
                            act.wait_ge(s_u, b * 32 + q - 2)
                        act.activation(pexp[q % 3], ps[:, 2 + q % 2, :], ACT.Exp).then_inc(s_pe, 1)
                    if q >= 2:
                        act.wait_ge(s_u, b * 32 + q - 1)
                        if q >= 4:
                            act.wait_ge(s_g, b * 32 + q - 3)
                        act.activation(pth[q % 2], pv_b[(q - 2) % 3], ACT.Tanh).then_inc(s_t, 1)
                act.wait_ge(s_c64, b + 1)
                for t in range(TT):
                    cols = e64[:, RH * t:RH * (t + 1), :]
                    act.activation(cols, cols, ACT.Silu, scale=hdc[:, t:t + 1], accum_out=wc[:, t:t + 1]).then_inc(s_wc, 1)
                sqrt(2)
                to_float(1, 1)
                turned(4, xnT[:, 0, :], 0)
                to_float(1, 0)
                for t in range(TT):
                    act.wait_ge(s_v, b * 8 + 4 + t + 1)
                    act.activation(v_aug[:, t, :, 0:DH], ps[:, 4 + t, 0:D].rearrange("p (h c) -> p h c", c=DH),
                                   ACT.Relu).then_inc(s_va, 1)
                attend(1)
                sqrt(3)
                act.wait_ge(s_tr, b * 6 + 6)
                for k in range(KC):
                    act.copy(xs[:, 0, k, :], ps[:, 4 + k, :]).then_inc(s_xh, 1)
                act.wait_ge(s_xl, b * 2 + 1)
                turned(5, xnT[:, 0, :], 4)
                sqrt(4)

                def w1_hi(e):
                    act.wait_ge(s_mw[e % 2], b * 64 + 16 * (e // 2 + 1))
                    if e == 1:
                        act.wait_ge(s_st, b * 64 + 64)
                    act.copy(w1s[e % 2][:, 0], w1b[e % 2]).then_inc(s_w1h, 1)

                def w2_hi(e):
                    act.wait_ge(s_mv[e % 2], b * 64 + 16 * (e // 2 + 1))
                    act.copy(w2s[e % 2][:, 0], w2b[e % 2]).then_inc(s_w2h, 1)

                act.wait_ge(s_w1h, b * ME + 1)
                w1_hi(1)
                for e in range(ME):
                    for f in range(MC):
                        act.wait_ge(s_mu, b * 32 + MC * e + f + 1)
                        if MC * e + f >= 2:
                            act.wait_ge(s_gl, b * 32 + MC * e + f - 1)
                        act.activation(g_raw[:, f % 2, :], ps[:, f, :], ACT.Gelu).then_inc(s_mg, 1)
                        if f == 0 and 2 <= e + 1 < ME:
                            w1_hi(e + 1)
                        if f == 2:
                            w2_hi(e)
                    if e == 0:
                        act.wait_ge(s_gm, b + 1)
                        act.activation(ee[:], lg2[:], ACT.Exp).then_inc(s_ge, 1)

        @block.tensor
        def _(pe):
            def turn(bank, src, rows=P):
                for k in range(KC):
                    for t in range(TT):
                        ins = pe.transpose(ps[:, bank + k, t * P:(t + 1) * P], src[:, t, k * P:(k + 1) * P], ident[:])
                return ins

            pe.wait_ge(s_w, 16 * 21)
            pe.wait_ge(s_ci, 16 * NCI)
            pe.wait_ge(s_ms, 1)
            for k in range(KC):
                for h in range(RH):
                    for half in range(2):
                        p = 1 - half
                        ins = pe.matmul(ps[:, k, (2 * h + half) * NK:(2 * h + half + 1) * NK],
                                        st_wq[:, RH * p + h, k * P:(k + 1) * P],
                                        st_keys[:, (2 * h + p) * NK:(2 * h + p + 1) * NK], start=True, stop=True)
                ins.then_inc(s_wret_ps, 1)
            pe.wait_ge(s_gi, 1)
            for i, src in enumerate((gw[:], lg[:, 0:KC, :])):
                for k in range(KC):
                    ins = pe.matmul(ps[:, 2 + i, 0:ME], ones[:], src[:, k, :], start=(k == 0), stop=(k == KC - 1))
            ins.then_inc(s_wret_ps, 1)
            pe.wait_ge(s_ms, 3 + SLOTS)
            pe.wait_ge(s_kbin, 16 * SLOTS)
            pe.wait_ge(s_conv, 5)
            pe.wait_ge(s_wret, 1)

            with pe.Fori(0, B) as b:
                def turned(i):
                    pe.wait_ge(s_tra, b * 6 + i + 1)
                    pe.wait_ge(s_trd, b * 6 + i + 1)

                def project(L, which):
                    w, src = (wq, wk)[which][L], (xnT, ctxT)[which]
                    for m in range(KC):
                        for k in range(KC):
                            ins = pe.matmul(ps[:, 2 * which + m, :], w[:, k, m * P:(m + 1) * P], src[:, k, :], start=(k == 0), stop=(k == KC - 1))
                        ins.then_inc(s_qk, 1)

                def project_v(L):
                    for t in range(TT):
                        for k in range(KC):
                            ins = pe.matmul(ps[:, 4 + t, 0:D], ctxT[:, k, t * P:(t + 1) * P], wv[L][:, k, :], start=(k == 0), stop=(k == KC - 1))
                        ins.then_inc(s_v, 1)

                def scores_by_key(L, u, half):
                    g, c = divmod(u, TT)
                    n = NG * L + g
                    s = n % SLOTS
                    if u == 0 and half == 0:
                        pe.wait_ge(s_va, b * 8 + 4 * L + 4)
                    if c == 0 and half == 0:
                        pe.wait_ge(s_mr[n % 2], b * 64 + 16 * (n // 2 + 1))
                    if u:
                        pe.wait_ge(s_e, b * 64 + 2 * (NU * L + u - 1) + half + 1)
                    for j in (2 * half, 2 * half + 1):
                        ins = pe.matmul(ps[:, 2 + j, :], stack_k[s][0:MROW + 1, j // 2, c * P:(c + 1) * P],
                                        stack_q[s][0:MROW + 1, j, :], start=True, stop=(L == 1))
                        if L == 0:
                            for i in range(2):
                                ins = pe.matmul(ps[:, 2 + j, c * P:(c + 1) * P], neg16[:, i, :], dist16[:], start=False, stop=(i == 1))
                    ins.then_inc(s_st, 1)

                def scores_by_query(L, v, t):
                    g, j = divmod(v, HG)
                    n = NG * L + g
                    s = n % SLOTS
                    if j % 2 == 0 and t == 0:
                        per, before = slot_turn(n)
                        pe.wait_ge(s_stk[s][j // 2], b * (per * STK[j // 2]) + (before + 1) * STK[j // 2])
                    if 4 * v + t >= 2:
                        pe.wait_ge(s_red, b * 128 + 64 * L + 4 * v + t - 1)
                    elif t == 1:
                        pe.wait_ge(s_qkf, b * 8 + 4 * L + 4)
                    pe.matmul(ps[:, t % 2, :], stack_q[s][0:MROW, j, t * P:(t + 1) * P],
                              stack_k[s][0:MROW, j // 2, :], start=True, stop=True).then_inc(s_s, 1)

                def values(L, u):
                    g, c = divmod(u, TT)
                    n = NG * L + g
                    pe.wait_ge(s_e, b * 64 + 2 * (NU * L + u) + 2)
                    if c == 0 and n:
                        pe.wait_ge(s_oT, b * 8 + n)
                    for j in range(HG):
                        ins = pe.matmul(ps[32 * j:32 * j + 32, 6, :], v_aug[:, c, HG * g + j, :],
                                        pt[:, 4 * (u % 2) + j, :], start=(c == 0), stop=(c == TT - 1))
                    ins.then_inc(s_pv, 1)

                def attend(L):
                    for u in range(-LEAD, NU + 2):
                        v = u + LEAD
                        for t in range(TT):
                            if t % 2 == 0 and 0 <= u < NU:
                                scores_by_key(L, u, t // 2)
                            if t == 1 and 1 <= u <= NU:
                                values(L, u - 1)
                            if v < NU:
                                scores_by_query(L, v, t)
                        if v > 0 and v % 4 == 0 and v <= NU:
                            n = NG * L + v // 4 - 1
                            pe.wait_ge(s_red, b * 128 + 16 * (n + 1))
                            if n == NG * L:
                                pe.wait_ge(s_va, b * 8 + 4 * L + 4)
                            if n - NG * L >= 2:
                                pe.wait_ge(s_on, b * 8 + n - 1)
                            pe.transpose(ps[0:HG * TT, 7, 0:P], negmax[:, n % 2, :], ident[:]).then_inc(s_mt, 1)
                        if u >= 5 and u % 4 == 1:
                            n = NG * L + (u - 5) // 4
                            pe.wait_ge(s_oT, b * 8 + n + 1)
                            if n >= 1:
                                pe.wait_ge(s_on, b * 8 + n)
                            pe.wait_ge(s_mc, b * 8 + min(NG * L + NG, n + 2))
                            for t in range(TT):
                                ins = pe.transpose(ps[:, 7, t * P:(t + 1) * P], oT[:, t * P:(t + 1) * P], ident[:])
                            ins.then_inc(s_ot, 1)

                pe.wait_ge(s_ctx, b * 16 + 16)
                turn(2, ctx_in).then_inc(s_tr, 1)
                turned(0)
                project(0, 1)
                pe.wait_ge(s_ln, b * 4 + 1)
                turn(0, xn).then_inc(s_tr, 1)
                turned(1)
                project(0, 0)
                project_v(0)
                attend(0)
                pe.wait_ge(s_on, b * 8 + 4)
                turn(0, xn).then_inc(s_tr, 1)
                turned(2)
                for t in range(TT):
                    for k in range(KC):
                        ins = pe.matmul(ps[:, 2 + t, 0:D], xnT[:, k, t * P:(t + 1) * P], wo[:, k, :], start=(k == 0), stop=(k == KC - 1))
                    ins.then_inc(s_wo, 1)
                pe.wait_ge(s_ln, b * 4 + 2)
                turn(0, xn).then_inc(s_tr, 1)
                turned(3)
                for t in range(TT):
                    for k in range(KC):
                        ins = pe.matmul(ps[:, 2 + t, :], xnT[:, k, t * P:(t + 1) * P], wret[:, k, :], start=(k == 0), stop=(k == KC - 1))
                    ins.then_inc(s_sim, 1)
                for t in range(TT):
                    for k in range(KC):
                        ins = pe.matmul(ps[:, 6, t:t + 1], xnT[:, k, t * P:(t + 1) * P], wdown_e[:, k, NE - 1:NE], start=(k == 0), stop=(k == KC - 1))
                ins.then_inc(s_hc, 1)
                def add_y(lhs, rhs, first, tiles=range(TT)):
                    for t in tiles:
                        ins = pe.matmul(ps[:, 6 + t // 2, (t % 2) * D:(t % 2 + 1) * D], lhs[:, t * P:(t + 1) * P], rhs,
                                        start=(first and t % 2 == 0), stop=True, skip_group_check=True)
                    return ins

                for f in range(FC + 1):
                    if f < FC:
                        if f >= 2:
                            pe.wait_ge(s_fs, b * 8 + f - 1)
                        for k in range(KC):
                            ins = pe.matmul(ps[:, f % 2, :], wff1[:, k, f * P:(f + 1) * P], xnT[:, k, :], start=(k == 0), stop=(k == KC - 1))
                        ins.then_inc(s_f, 1)
                    if f >= 1:
                        if f == 1:
                            pe.wait_ge(s_hcc, b + 1)
                        pe.wait_ge(s_fs, b * 8 + f)
                        add_y(ffh[:, (f - 1) % 2, :], wff2[:, f - 1, :], f == 1).then_inc(s_fd, 1)
                def expert_products(c, k):
                    if c >= 2 and k == 0:
                        pe.wait_ge(s_hdc, b * 8 + c - 1)
                    ins = pe.matmul(ps[:, c % 2, :], wdown_e[:, k, c * P:(c + 1) * P], xnT[:, k, :], start=(k == 0), stop=(k == KC - 1))
                    if k == KC - 1:
                        ins.then_inc(s_hd, 1)

                for c, k in ((0, 0), (0, 1), (1, 0)):
                    expert_products(c, k)
                pe.wait_ge(s_row, b + 1)
                for h in range(RH):
                    for t in range(TT):
                        ins = pe.transpose(ps[0:TROWS, 2 + h, t * P:(t + 1) * P], simcat[:, t, h, 0:TROWS], ident[:])
                    ins.then_inc(s_tt, 1)
                pe.wait_ge(s_th, b * 4 + 4)
                pe.wait_ge(s_tl, b * 4 + 4)
                for q in range(RH * EC + 7):
                    c, h = divmod(q, RH)
                    if q < RH * EC:
                        for i0, base, done, mine in ((0, 2, s_pe, s_l), (1, 4, s_pm, s_m)):
                            if q >= 2:
                                pe.wait_ge(done, b * 32 + q - 1)
                            for i in range(2):
                                ins = pe.matmul(ps[:, base + q % 2, :], sel[:, c, i0, :], tr[:, 2 * h + i, :], start=(i == 0), stop=(i == 1))
                            ins.then_inc(mine, 1)
                        if h == 1 and c + 1 < EC:
                            expert_products(c + 1, 1)
                        if h == 3 and c + 2 < EC:
                            expert_products(c + 2, 0)
                    if c >= 2 and h < 3:
                        if h == 0:
                            pe.wait_ge(s_acc, b * 8 + c - 1)
                        ins = add_y(acc[:, c % 2, :], wup_e[:, c - 2, :], False, ((0,), (1,), (2, 3))[h])
                        if h == 2:
                            ins.then_inc(s_yu, 1)
                project(1, 1)
                pe.wait_ge(s_ln, b * 4 + 3)
                turn(0, xn).then_inc(s_tr, 1)
                turned(4)
                project(1, 0)
                project_v(1)
                attend(1)
                pe.wait_ge(s_ln, b * 4 + 4)
                turn(4, xn).then_inc(s_tr, 1)

                def products(dst, lhs, rhs, first, last):
                    for i, j in ((0, 0), (0, 1), (1, 0)):
                        ins = pe.matmul(dst, lhs(i), rhs(j), start=(first and i == j), stop=(last and i == 1))
                    return ins

                def expert_up(e, tiles=range(MC)):
                    pe.wait_ge(s_w1s, b * ME + e + 1)
                    for f in tiles:
                        if e:
                            pe.wait_ge(s_mg, b * 32 + MC * (e - 1) + f + 1)
                        for k in range(KC):
                            ins = products(ps[:, f, :], lambda i: w1s[e % 2][:, i, k, f * P:(f + 1) * P], lambda j: xs[:, j, k, :],
                                           k == 0, k == KC - 1)
                        ins.then_inc(s_mu, 1)

                def expert_down(e, f):
                    pe.wait_ge(s_gl, b * 32 + MC * e + f + 1)
                    if f == 0:
                        pe.wait_ge(s_w2s, b * ME + e + 1)
                    for t in range(TT):
                        if f == 0 and e >= 1:
                            pe.wait_ge(s_ma, b * 32 + 4 * (e - 1) + t + 1)
                        elif f == 0 and t == 3:
                            pe.wait_ge(s_gm, b + 1)
                        ins = products(ps[:, 4 + t, 0:D], lambda i: gs[f][:, i, t * P:(t + 1) * P], lambda j: w2s[e % 2][:, j, f, :],
                                       f == 0, f == MC - 1)
                        if f == MC - 1:
                            ins.then_inc(s_md, 1)
                    if f < MC - 1:
                        ins.then_inc(s_mf, 1)

                pe.wait_ge(s_xl, b * 2 + 2)
                expert_up(0, (0, 1))
                turned(5)
                pe.wait_ge(s_on, b * 8 + 8)
                for t in range(TT):
                    for k in range(KC):
                        ins = pe.matmul(ps[:, 7, t * ME:(t + 1) * ME], xnT[:, k, t * P:(t + 1) * P], gw[:, k, :], start=(k == 0), stop=(k == KC - 1))
                ins.then_inc(s_gp, 1)
                expert_up(0, (2, 3))
                for e in range(1, ME + 1):
                    for f in range(MC):
                        if e < ME:
                            expert_up(e, (f,))
                        expert_down(e - 1, f)

        @block.vector
        def _(dve):
            own = Own(dve, s_owni, 0, 0)
            dve.wait_ge(s_ci, 16 * NCI)
            dve.tensor_copy(kb_c, st_kb).then_inc(s_conv, 1)
            dve.tensor_copy(qb_c[:, 0, :], st_qb).then_inc(s_conv, 1)
            dve.tensor_scalar(qb_c[:, 1, :], st_qb, 0.0, None, ALU.mult).then_inc(s_conv, 1)
            dve.tensor_copy(sel[:].rearrange("p c i m -> p (c i m)"), st_sel).then_inc(s_conv, 1)
            own(dve.tensor_copy(neg16[:, 0, :], st_neg))
            own(dve.tensor_copy(dist16[:], st_dist))
            dve.wait_ge(s_owni, own.k)
            own(dve.tensor_tensor(st_negh, st_neg, neg16[:, 0, :], ALU.subtract))
            dve.wait_ge(s_owni, own.k)
            own(dve.tensor_copy(neg16[:, 1, :], st_negh))
            dve.wait_ge(s_w, 16 * 21)
            for k in range(KC):
                own(dve.tensor_scalar(lg[:, k, :], gw[:, k, :], gcol[:, KC + k:KC + k + 1], None, ALU.mult))
            dve.wait_ge(s_owni, own.k)
            for k in range(KC):
                own(dve.tensor_scalar(gw[:, k, :], gw[:, k, :], gcol[:, k:k + 1], None, ALU.mult))
            dve.wait_ge(s_owni, own.k)
            dve.tensor_scalar(bqk[:, 0, :], bqk[:, 0, :], SCALE, None, ALU.mult).then_inc(s_conv, 1)
            dve.wait_ge(s_conv, 5)
            dve.sem_inc(s_gi, 1)
            for k in range(KC):
                dve.wait_ge(s_wret_ps, k + 1)
                own(dve.tensor_copy(wret[:, k, :], ps[:, k, :]))
            dve.wait_ge(s_wret_ps, KC + 1)
            for i in range(2):
                own(dve.tensor_copy(gbc[:, i, :], ps[:, 2 + i, 0:ME]))
            dve.wait_ge(s_owni, own.k)
            dve.sem_inc(s_wret, 1)

            with dve.Fori(0, B) as b:
                own = Own(dve, s_own, OWN_STEPS, b)

                def stats(i, src):
                    for t in range(TT):
                        own(dve.bn_stats(st6[:, t, :], src[:, t, :]))
                    own.wait(alone=True)
                    for t in range(TT):
                        own(dve.bn_aggr(mv[:, t, :], st6[:, t, :]))
                    own.wait()
                    dve.tensor_scalar(ve[:], mv[:, :, 1], EPS, None, ALU.add).then_inc(s_lnv, 1)
                    dve.wait_ge(s_lnd, b * 5 + i + 1)
                    own(dve.reciprocal(rstd[:], sd[:]))
                    own.wait()

                def layernorm(i, src):
                    stats(i, src)
                    for t in range(TT):
                        ins = dve.tensor_scalar(xn[:, t, :], src[:, t, :], mv[:, t, 0:1], rstd[:, t:t + 1], ALU.subtract, ALU.mult)
                        if t < TT - 1:
                            own(ins)
                    own.wait()
                    ins.then_inc(s_ln, 1)

                def turned(i, dst, bank):
                    dve.wait_ge(s_tr, b * 6 + i + 1)
                    dve.tensor_copy(dst, ps[:, bank, :]).then_inc(s_trd, 1)

                def split_qk(L):
                    dve.wait_ge(s_qkf, b * 8 + 4 * L + 2)
                    for m in range(KC):
                        own(dve.tensor_copy(ks[:, 0, m, :], kf[:, m, :]))
                        own.wait()
                        own(dve.tensor_tensor(ks[:, 1, m, :], kf[:, m, :], ks[:, 0, m, :].bitcast(F32), ALU.subtract))
                    for m in range(KC):
                        dve.wait_ge(s_qkf, b * 8 + 4 * L + 2 + m + 1)
                        for h in range(2):
                            own(dve.tensor_scalar(qs[:, 0, m, h, :], qf[:, m, :], par[:, h:h + 1], None, ALU.mult))
                        own.wait()
                        for h in range(2):
                            ins = dve.scalar_tensor_tensor(out=qs[:, 1, m, h, :], in0=qf[:, m, :], scalar=par[:, h:h + 1],
                                                           in1=qs[:, 0, m, h, :].bitcast(F32), op0=ALU.mult, op1=ALU.subtract)
                        ins.then_inc(s_split, 1)

                def attend(L):
                    for u in range(-LEAD, NU + 2):
                        v = u + LEAD
                        if 0 <= v < NU:
                            g, j = divmod(v, HG)
                            n = NG * L + g
                            if j == 0 and n >= 2:
                                dve.wait_ge(s_mt, b * 8 + n - 1)
                            for t in range(TT):
                                dve.wait_ge(s_s, b * 128 + 64 * L + 4 * v + t + 1)
                                dve.tensor_reduce(negmax[:, n % 2, 4 * j + t:4 * j + t + 1], ps[:, t % 2, :], AX, ALU.max, negate=True).then_inc(s_red, 1)
                        if u >= 5 and u % 4 == 1:
                            g = (u - 5) // 4
                            n = NG * L + g
                            dve.wait_ge(s_ot, b * 8 + n + 1)
                            o4 = ps[:, 7, :].rearrange("p (t j c) -> p t j c", t=TT, j=HG)
                            own(dve.reciprocal(rec[:], o4[:, :, :, DH]))
                            own.wait()
                            dst = xn[:, :, 64 * g:64 * (g + 1)].rearrange("p t (j c) -> p t j c", c=DH)
                            dve.tensor_tensor(dst, o4[:, :, :, 0:DH], rec[:].unsqueeze(3).broadcast_to([P, TT, HG, DH]), ALU.mult).then_inc(s_on, 1)
                            if L == 1:
                                dve.wait_ge(s_on, b * 8 + n + 1)
                                cols = slice(64 * g, 64 * (g + 1))
                                own(dve.tensor_tensor(x_tok[:, :, cols], x_tok[:, :, cols], xn[:, :, cols], ALU.add))

                dve.wait_ge(s_x, b * 16 + 16)
                turned(0, ctxT[:, 1, :], 3)
                layernorm(0, x_in)
                turned(1, xnT[:, 1, :], 1)
                split_qk(0)
                dve.wait_ge(s_ms, 3 + SLOTS)
                for t in range(TT):
                    dve.wait_ge(s_v, b * 8 + t + 1)
                    dve.tensor_tensor(v_aug[:, t, :, 0:DH], ps[:, 4 + t, 0:D].rearrange("p (h c) -> p h c", c=DH),
                                      bv_bc[:].rearrange("p (h c) -> p h c", c=DH), ALU.add).then_inc(s_va, 1)
                attend(0)
                turned(2, xnT[:, 1, :], 1)
                dve.wait_ge(s_xb, b + 1)
                for t in range(TT):
                    dve.wait_ge(s_wo, b * 4 + t + 1)
                    dve.tensor_tensor(x_tok[:, t, :], ps[:, 2 + t, 0:D], x_in[:, t, :], ALU.add).then_inc(s_x1, 1)
                dve.wait_ge(s_x1, b * 4 + 4)
                layernorm(1, x_tok)
                turned(3, xnT[:, 1, :], 1)
                for t in range(TT):
                    dve.wait_ge(s_simc, b * 4 + t + 1)
                    dve.nop(nofuse=True)
                    for h in range(RH):
                        own(dve.max(sy8[:, RH * t + h, :], simcat[:, t, h, 0:NK]))
                        own(dve.max(sx8[:, RH * t + h, :], simcat[:, t, h, NK:2 * NK]))
                own.wait(alone=True)
                for t in range(TT):
                    for h in range(RH):
                        own(dve.max_index(ix8[:, RH * t + h, :], sx8[:, RH * t + h, :], simcat[:, t, h, NK:2 * NK]))
                R = TT * RH
                own(dve.tensor_tensor(s64.rearrange("p a (i j) -> p a i j", j=8), sx8[:].unsqueeze(3).broadcast_to([P, R, 8, 8]),
                                      sy8[:].unsqueeze(2).broadcast_to([P, R, 8, 8]), ALU.add))
                own(dve.tensor_reduce(mag[:, 0, :], sx8[:], AX, ALU.add, apply_absolute_value=True))
                own(dve.tensor_reduce(mag[:, 1, :], sy8[:], AX, ALU.add, apply_absolute_value=True))
                own.wait()
                own(dve.tensor_scalar(ixg[:], ix8[:], float(NX), None, ALU.is_ge))
                own(dve.tensor_tensor(mag[:, 0, :], mag[:, 0, :], mag[:, 1, :], ALU.add))
                for r in range(R):
                    own(dve.max(v8[:, r, :], s64[:, r, :]))
                own.wait()
                own(dve.tensor_tensor(c64[:], s64, v8[:, :, 7:8].broadcast_to([P, R, 64]), ALU.is_ge))
                own(dve.scalar_tensor_tensor(out=simcat.rearrange("p t h c -> p (t h) c")[:, :, R_THR], in0=mag[:, 0, :], scalar=DELTA,
                                             in1=v8[:, :, 7], op0=ALU.mult, op1=ALU.subtract))
                own(dve.tensor_copy(zz[:], v8[:, :, 0]))
                own.wait()
                dve.tensor_tensor(v8[:], v8[:], zz[:].unsqueeze(2).broadcast_to([P, R, 8]), ALU.subtract).then_inc(s_d8, 1)
                own(dve.tensor_tensor(c64[:].rearrange("p a (i j) -> p (a i) j", j=8), c64[:].rearrange("p a (i j) -> p (a i) j", j=8),
                                      ixg[:].rearrange("p a i -> p (a i)").unsqueeze(2).broadcast_to([P, R * 8, 8]), ALU.mult))
                own(dve.tensor_copy(mag[:, 1, :], zz[:]))
                own.wait()
                dve.wait_ge(s_e8, b + 1)
                dve.tensor_reduce(zz[:], e8[:], AX, ALU.add).then_inc(s_z8, 1)
                dve.wait_ge(s_l8, b + 1)
                dve.scalar_tensor_tensor(out=simcat.rearrange("p t h c -> p (t h) c")[:, :, R_LOGIT], in0=lnz[:], scalar=-1.0,
                                         in1=mag[:, 1, :], op0=ALU.mult, op1=ALU.subtract).then_inc(s_row, 1)
                dve.wait_ge(s_row, b + 1)
                dve.tensor_tensor(e64, s64, simcat.rearrange("p t h c -> p (t h) c")[:, :, R_LOGIT:R_LOGIT + 1].broadcast_to([P, R, 64]),
                                  ALU.add).then_inc(s_a64, 1)
                for h in range(RH):
                    dve.wait_ge(s_th, b * 4 + h + 1)
                    dve.tensor_tensor(tr[:, 2 * h + 1, :], ps[0:TROWS, 2 + h, :], tr[:, 2 * h, :].bitcast(F32), ALU.subtract).then_inc(s_tl, 1)
                dve.wait_ge(s_x64, b + 1)
                dve.tensor_tensor(e64, e64, c64[:], ALU.mult).then_inc(s_c64, 1)
                for q in range(EC * RH + 3):
                    if q < EC * RH:
                        dve.wait_ge(s_m, b * 32 + q + 1)
                        dve.wait_ge(s_pe, b * 32 + q + 1)
                        dve.scalar_tensor_tensor(out=pexp[q % 3], in0=ps[:, 4 + q % 2, :], scalar=0.0, in1=pexp[q % 3],
                                                 op0=ALU.is_ge, op1=ALU.mult).then_inc(s_pm, 1)
                    if q >= 3:
                        c, h = divmod(q - 3, RH)
                        dve.wait_ge(s_t, b * 32 + q - 2)
                        if h == 0 and c >= 2:
                            dve.wait_ge(s_yu, b * 8 + c - 1)
                        if h == 1 and c:
                            dve.wait_ge(s_acc, b * 8 + c)
                        dst = acc[:, c % 2, :] if h == 0 else wt[:, h % 2, :]
                        dve.scalar_tensor_tensor(out=dst, in0=pth[(q - 3) % 2], scalar=1.0, in1=pv_b[(q - 3) % 3],
                                                 op0=ALU.add, op1=ALU.mult).then_inc(s_g, 1)
                        if h:
                            dve.wait_ge(s_g, b * 32 + q - 2)
                            if h > 1:
                                own.wait()
                            ins = dve.tensor_tensor(acc[:, c % 2, :], acc[:, c % 2, :], dst, ALU.add)
                            if h == RH - 1:
                                ins.then_inc(s_acc, 1)
                            else:
                                own(ins)
                dve.wait_ge(s_yu, b * 8 + 8)
                dve.wait_ge(s_wc, b * 4 + 4)
                for i in range(2):
                    own(dve.tensor_tensor(x_tok[:, 2 * i:2 * i + 2, :].rearrange("p t d -> p (t d)"), ps[:, 6 + i, :],
                                          x_tok[:, 2 * i:2 * i + 2, :].rearrange("p t d -> p (t d)"), ALU.add))
                own.wait()
                for t in range(TT):
                    own(dve.scalar_tensor_tensor(out=x_tok[:, t, :], in0=last_up[:], scalar=wc[:, t:t + 1], in1=x_tok[:, t, :],
                                                 op0=ALU.mult, op1=ALU.add))
                own.wait()
                layernorm(2, x_tok)
                turned(4, xnT[:, 1, :], 1)
                split_qk(1)
                attend(1)
                own.wait()
                layernorm(3, x_tok)
                for k in range(KC):
                    dve.wait_ge(s_xh, b * 2 + k + 1)
                    dve.tensor_tensor(xs[:, 1, k, :], ps[:, 4 + k, :], xs[:, 0, k, :].bitcast(F32), ALU.subtract).then_inc(s_xl, 1)
                turned(5, xnT[:, 1, :], 5)
                dve.wait_ge(s_ln, b * 4 + 4)
                stats(4, xn)
                own(dve.tensor_tensor(lg2[:], gbc[:, 0, :].unsqueeze(1).broadcast_to([P, TT, ME]), mv[:, :, 0:1].broadcast_to([P, TT, ME]), ALU.mult))
                own.wait()
                dve.wait_ge(s_gp, b + 1)
                own(dve.tensor_tensor(lg[:], ps[:, 7, 0:TT * ME].rearrange("p (t e) -> p t e", e=ME), lg2[:], ALU.subtract))
                own.wait()
                own(dve.tensor_tensor(lg[:], lg[:], rstd[:].unsqueeze(2).broadcast_to([P, TT, ME]), ALU.mult))
                own.wait()
                own(dve.tensor_tensor(lg[:], lg[:], gbc[:, 1, :].unsqueeze(1).broadcast_to([P, TT, ME]), ALU.add))
                own.wait(alone=True)
                for t in range(TT):
                    own(dve.max(mx8[:, t, :], lg[:, t, :]))
                own.wait()
                dve.tensor_tensor(lg2[:], lg[:], mx8[:, :, 0:1].broadcast_to([P, TT, ME]), ALU.subtract).then_inc(s_gm, 1)
                own(dve.tensor_tensor(comb[:], lg[:], mx8[:, :, 1:2].broadcast_to([P, TT, ME]), ALU.is_ge))

                def gate():
                    dve.wait_ge(s_ge, b + 1)
                    own(dve.tensor_reduce(gz[:], ee[:], AX, ALU.add))
                    own.wait()
                    own(dve.reciprocal(gz[:], gz[:]))
                    own(dve.tensor_tensor(comb[:], comb[:], ee[:], ALU.mult))
                    own.wait()
                    own(dve.tensor_tensor(comb[:], comb[:], gz[:].unsqueeze(2).broadcast_to([P, TT, ME]), ALU.mult))
                    own.wait()

                for e in range(ME + 1):
                    for f in range(MC):
                        if e and f == MC - 1:
                            for t in range(TT):
                                dve.wait_ge(s_md, b * 32 + 4 * (e - 1) + t + 1)
                                if e >= 2:
                                    dve.wait_ge(s_ma, b * 32 + 4 * (e - 2) + t + 1)
                                dve.scalar_tensor_tensor(out=x_tok[:, t, :], in0=ps[:, 4 + t, 0:D], scalar=comb[:, t, e - 1:e],
                                                         in1=x_tok[:, t, :], op0=ALU.mult, op1=ALU.add).then_inc(s_ma, 1)
                        if e < ME:
                            hi, lo = (gs[f][:, i, :] for i in range(2))
                            dve.wait_ge(s_mg, b * 32 + MC * e + f + 1)
                            if e and f < MC - 1:
                                dve.wait_ge(s_mf, b * 24 + (MC - 1) * (e - 1) + f + 1)
                            own(dve.tensor_copy(hi, g_raw[:, f % 2, :]))
                            own.wait()
                            dve.tensor_tensor(lo, g_raw[:, f % 2, :], hi.bitcast(F32), ALU.subtract).then_inc(s_gl, 1)
                    if e == 0:
                        gate()
                own.close()


OWN_STEPS = 226


def layout(i):
    c = np.ascontiguousarray
    f = lambda n: np.asarray(i[n])
    cols = lambda n: c(f(n).reshape(KC, P).T)
    return {
        "x": c(f("x")), "ctx": c(f("ctx_1024")),
        "wq0": c(f("L0_xattn_Wq").T), "wk0": c(f("L0_xattn_Wk").T), "wv0": c(f("L0_xattn_Wv").T), "wo0": c(f("L0_xattn_Wo").T),
        "bq": cols("L0_xattn_bq"), "bk": cols("L0_xattn_bk"), "bv": c(f("L0_xattn_bv")), "bo": c(f("L0_xattn_bo")),
        "w_ret": c(f("L0_ffn_W_q")), "keys": c(f("L0_ffn_keys").transpose(3, 0, 2, 1)),
        "down_e": c(f("L0_ffn_down_embed").T), "up_e": c(f("L0_ffn_up_embed")),
        "ff1": c(f("L0_ffn_W_up").T), "ff2": c(f("L0_ffn_W_down").T),
        "wq1": c(f("L1_xattn_Wq").T), "wk1": c(f("L1_xattn_Wk").T), "wv1": c(f("L1_xattn_Wv").T),
        "gate": c(f("L1_ffn_gate_w").T), "gamma": cols("L1_ffn_ln_gamma"), "beta": cols("L1_ffn_ln_beta"),
        "w1": c(f("L1_ffn_w1").transpose(0, 2, 1)), "w2": c(f("L1_ffn_w2").transpose(0, 2, 1)),
    }


def kernel(**inputs):
    import concourse.bacc as bacc
    from concourse.bass_utils import run_bass_kernel_spmd

    nc = bacc.Bacc("TRN2", target_bir_lowering=False, num_devices=1, dynamic_dma_scratch_size=8192)
    arrays = {**layout(inputs), **shape_constants()}
    aps = {k: nc.dram_tensor("in_" + k, v.shape, mybir.dt.from_np(v.dtype), kind="ExternalInput").ap() for k, v in arrays.items()}
    out = nc.dram_tensor("out", (B, T, D), F32, kind="ExternalOutput").ap()
    build(nc, aps, out)
    r = run_bass_kernel_spmd(nc, [{"in_" + k: v for k, v in arrays.items()}], core_ids=[0])
    return r.results[0]["out"]
```

```python
from contextlib import ExitStack

import numpy as np

import concourse.bass as bass
from concourse import mybir

ALU = mybir.AluOpType
ACT = mybir.ActivationFunctionType
AX = mybir.AxisListType.X
F32 = mybir.dt.float32
F32R = mybir.dt.float32r
F16 = mybir.dt.float16
U32 = mybir.dt.uint32

P = 128
B, T, D = 4, 512, 256
TT, KC = T // P, D // P
H, DH = 16, 16
HG = 4
NG = H // HG
NU = NG * TT
SCALE = DH ** -0.5
SLOTS = 3
PR = 2 * DH
BROW = 3 * PR
NB = 2 * TT
MROW = BROW + NB
BIAS, UNITS = 0.1, 10
ORDER = (("key", 0), ("query", 0), ("query", 1), ("key", 1), ("query", 2), ("values", 0), ("query", 3))
LEAD = 6

FF = 1024
FC = FF // P
NE = 1024
EC = NE // P
RH, NK, RD = 4, 64, 64
NX = NE // NK
TROWS = 96
R_LOGIT, R_THR = NK + NX, NK + NX + 1
DELTA = 2.0 ** -22
TBANK = (2, 4, 3, 5)
RING = 4

ME, MF = 8, 512
MC = MF // P
EPS = 1e-5


def shape_constants():
    k = np.arange(T)
    kb, qb = np.zeros((NB, T), np.float32), np.zeros((NB, T), np.float32)
    for c in range(TT):
        here = (k // P == c)
        kb[2 * c] = np.where(here, -1, 0)
        kb[2 * c + 1] = np.where(here, k - P * c, 0)
        qb[2 * c] = np.where(here, 0, np.abs(k - P * c))
        qb[2 * c + 1] = np.sign(k // P - c)
    i = np.arange(P)
    sel = np.zeros((TROWS, EC, 2, P), np.float32)
    for c in range(EC):
        sel[i % NK, c, :, i] = 1
        sel[NK + 2 * c + i // NK, c, :, i] = 1
        sel[R_LOGIT, c, 0, i] = 1
        sel[R_THR, c, 1, i] = 1
    return {
        "c_ident": np.eye(P, dtype=np.float32),
        "c_dist": np.abs(i[:, None] - i[None, :]).astype(np.float32),
        "c_kb": kb, "c_qb": np.stack([qb, 0 * qb], 1),
        "c_par": np.stack([(i // DH) % 2 == 0, (i // DH) % 2 == 1], 1).astype(np.float32),
        "c_sel": sel.reshape(TROWS, -1),
    }


class Own:

    def __init__(self, eng, sem, n, b):
        self.eng, self.sem, self.n, self.b, self.k = eng, sem, n, b, 0

    def __call__(self, ins):
        ins.then_inc(self.sem, 1)
        self.k += 1

    def wait(self, alone=False):
        self.eng.wait_ge(self.sem, self.b * self.n + self.k)
        if alone:
            self.eng.nop(nofuse=True)

    def close(self):
        assert self.k == self.n, (self.k, self.n)


def build(nc, a, out):
    ctx = ExitStack()
    with ctx:
        sb = lambda name, shape, dt=F32: ctx.enter_context(nc.sbuf_tensor(name, shape, dt))
        sem = lambda name: ctx.enter_context(nc.semaphore(name))

        wq = [sb(f"wq{l}", [P, KC, D]) for l in range(2)]
        wk = [sb(f"wk{l}", [P, KC, D]) for l in range(2)]
        wv = [sb(f"wv{l}", [P, KC, D]) for l in range(2)]
        wo = sb("wo", [P, KC, D])
        wret = sb("wret", [P, KC, RH * 2 * NK])
        wdown_e = sb("wdown_e", [P, KC, NE])
        wup_e = sb("wup_e", [P, EC, D])
        wff1 = sb("wff1", [P, KC, FF])
        wff2 = sb("wff2", [P, FC, D])
        gw = sb("gw", [P, KC, ME])
        gcol = sb("gcol", [P, 2 * KC])
        gbc = sb("gbc", [P, 2, ME])
        bqk = sb("bqk", [P, 2, KC])
        bv_bc = sb("bv_bc", [P, D])
        bo_bc = sb("bo_bc", [P, D])
        last_up = sb("last_up", [P, D])
        ident = sb("ident", [P, P])
        ones = sb("ones", [P, P])
        neg16 = sb("neg16", [P, P], F16)
        dist16 = sb("dist16", [P, P], F16)
        sel = sb("sel", [TROWS, EC, 2, P], F32R)
        qb_c = sb("qb_c", [NB, 2, T], F32R)
        x_in = sb("x_in", [P, TT, D])
        ctx_in = sb("ctx_in", [P, TT, D])
        x_tok = sb("x_tok", [P, TT, D])
        xn = sb("xn", [P, TT, D])
        xnT = sb("xnT", [P, KC, T])
        ctxT = sb("ctxT", [P, KC, T])
        v_aug = sb("v_aug", [P, TT, H, 32])
        par = sb("par", [P, 2])
        qs = sb("qs", [P, 2, KC, 2, T], F32R)
        ks = sb("ks", [P, 2, KC, T], F32R)
        pt = sb("pt", [P, 8, T])
        moe_w = sb("moe_w", [P, 2, 2 * MC * D])
        g_parts = sb("g_parts", [P, 4, T], F32R)
        oT = sb("oT", [P, T])
        stack_q = [sb(f"stack_q{s}", [P, HG, T], F32R) for s in range(SLOTS)]
        stack_k = [sb(f"stack_k{s}", [MROW + 1, HG // 2, T], F32R) for s in range(SLOTS)]
        negmax = sb("negmax", [P, 2, HG * TT])
        m_sb = sb("m_sb", [HG * TT, 2, P], F32R)
        rec = sb("rec", [P, TT, HG])
        st6 = sb("st6", [P, TT, 6])
        mv = sb("mv", [P, TT, 2])
        eps = sb("eps", [P, 1])
        scratch = sb("scratch", [P, 1])
        sd = sb("sd", [P, TT])
        rstd = sb("rstd", [P, TT])
        ffh = sb("ffh", [P, 2, T])
        sx8 = sb("sx8", [P, TT * RH, 8])
        sy8 = sb("sy8", [P, TT * RH, 8])
        ix8 = sb("ix8", [P, TT * RH, 8], U32)
        ixg = sb("ixg", [P, TT * RH, 8])
        v8 = sb("v8", [P, TT * RH, 8])
        e8 = sb("e8", [P, TT * RH, 8])
        zz = sb("zz", [P, TT * RH])
        lnz = sb("lnz", [P, TT * RH])
        mag = sb("mag", [P, 2, TT * RH])
        hdc = sb("hdc", [P, TT])
        wc = sb("wc", [P, TT])
        c64 = sb("c64", [P, TT * RH, 64])
        lg = sb("lg", [P, TT, ME])
        lg2 = sb("lg2", [P, TT, ME])
        mx8 = sb("mx8", [P, TT, 8])
        ee = sb("ee", [P, TT, ME])
        gz = sb("gz", [P, TT])
        comb = sb("comb", [P, TT, ME])
        simcat = moe_w[:, 0, :].rearrange("p (t h c) -> p t h c", t=TT, h=RH)
        s64 = moe_w[:, 1, 0:1024].rearrange("p (a c) -> p a c", c=64)
        e64 = moe_w[:, 1, 1024:2048].rearrange("p (a c) -> p a c", c=64)
        tr = qs[0:TROWS].rearrange("p i k h t -> p (i k h) t")
        pexp = [pt[:, i, :] for i in range(RING)]
        pv_b = [pt[:, RING + i, :] for i in range(RING)]
        pth = [ffh[:, i, :] for i in range(2)]
        qf, kf = pt[:, 0:2, :], pt[:, 2:4, :]
        two = lambda buf: buf[:].rearrange("p (a b) d -> p a (b d)", a=2)
        hdT, acc, wt = two(x_in), two(ctx_in), two(xn)
        flat = lambda buf: buf[:].rearrange("p a b -> p (a b)")
        parts = lambda v: v.rearrange("p (i t) -> p i t", i=2)
        qs_flat = qs[:].rearrange("p i k h t -> p (i k h t)")
        xs = ks
        ff1s = [flat(stack_q[i]).rearrange("p (k n) -> p k n", k=KC) for i in range(2)]
        downs = [flat(buf).rearrange("p (k n) -> p k n", k=KC) for buf in (stack_q[2], g_parts)]
        w1s = [v.rearrange("p (i k f) -> p i k f", i=2, k=KC) for v in (qs_flat[:, 0:2 * KC * MF], flat(stack_q[0]))]
        w2s = [v.rearrange("p (i k f) -> p i k f", i=2, k=MC) for v in (qs_flat[:, 2 * KC * MF:], flat(stack_q[1]))]
        gs = [parts(flat(buf)[:, 2 * T * f:2 * T * (f + 1)]) for buf in (stack_q[2], g_parts) for f in range(2)]
        g_raw = two(xn)
        w1b = [moe_w[:, s, 0:1024].rearrange("p (k f) -> p k f", k=KC) for s in range(2)]
        w2b = [moe_w[:, s, 1024:2048].rearrange("p (k f) -> p k f", k=MC) for s in range(2)]
        kb_c = g_parts[0:NB, 0, :]
        st_sel = moe_w[0:TROWS, 0, :]
        st_kb, st_qb = pt[0:NB, 4, :], pt[0:NB, 5:7, :]
        st_dist = pt[:, 7, 0:P]
        st_wq = moe_w[0:RD, 0, :].rearrange("p (a d) -> p a d", d=D)
        st_keys = moe_w[0:RD, 1, 0:RH * 2 * NK]

        ps = ctx.enter_context(nc.psum_tensor("ps", [P, 8, 512], F32))

        v_psum = lambda L, t: (ps[:, 4 + t, 0:D], ps[:, 6 + t // 2, (t % 2) * D:(t % 2 + 1) * D])[L]
        max_banks = lambda v: 4 if v < LEAD else 2
        slot_turn = lambda n: (len(range(n % SLOTS, 2 * NG, SLOTS)), n // SLOTS)

        s_w = sem("weights_in"); s_late = sem("late_weights_in"); s_ci = sem("consts_in")
        s_selin = sem("selector_in"); s_sel = sem("selector_ready")
        s_conv = sem("consts_ready"); s_ms = sem("memsets_done"); s_wret_ps = sem("wret_psum")
        s_wret = sem("wret_ready"); s_gi = sem("gate_psum"); s_kbin = sem("bias_rows_in")
        s_x = sem("x_in"); s_ctx = sem("ctx_in")
        s_lnv = sem("ln_var"); s_lnd = sem("ln_sd")
        s_ln = sem("ln_out")
        s_tr = sem("transposes_psum")
        s_tra = sem("transposed_act"); s_trd = sem("transposed_dve")
        s_qk = sem("qk_psum"); s_qkf = sem("qk_float")
        s_ksplit = sem("k_split"); s_qsplit = sem("q_split")
        s_v = sem("v_psum"); s_va = sem("v_ready")
        s_stk = [[sem(f"stack_in{s}_{i}") for i in range(HG // 2)] for s in range(SLOTS)]
        s_s = sem("scores_psum"); s_red = sem("max_reduced")
        s_mt = sem("max_turned"); s_mc = sem("max_copied")
        s_mr = [sem(f"max_rows_in{i}") for i in range(2)]
        s_st = sem("scoresT_psum"); s_e = sem("probs_ready")
        s_pv = sem("pv_psum"); s_oT = sem("o_copied")
        s_ot = sem("o_turned"); s_on = sem("o_normed")
        s_wo = sem("wo_psum"); s_x1 = sem("x1_added")
        s_xb = sem("x_plus_bo")
        s_sim = sem("sim_psum"); s_simc = sem("sim_copied")
        s_hc = sem("hd_last_psum"); s_hcc = sem("hd_last_copied")
        s_f = sem("ff_psum"); s_fs = sem("ff_silu"); s_fd = sem("ff_down")
        s_d8 = sem("top8_shifted"); s_e8 = sem("top8_exp")
        s_z8 = sem("top8_sum"); s_l8 = sem("top8_log")
        s_a64 = sem("pairs_shifted"); s_x64 = sem("pairs_exp")
        s_c64 = sem("pairs_masked"); s_wc = sem("clamped_weight")
        s_row = sem("sim_rows_ready"); s_tt = sem("sim_turned")
        s_th = sem("sim_hi"); s_tl = sem("sim_lo")
        s_hd = sem("hd_psum"); s_hdc = sem("hd_copied")
        s_l = sem("logit_psum"); s_m = sem("mask_psum")
        s_pe = sem("p_exp"); s_pm = sem("p_masked")
        s_u = sem("u_ready"); s_t = sem("tanh_ready"); s_g = sem("gated")
        s_fh = sem("ff_hi"); s_fl = sem("ff_split")
        s_a01 = sem("two_heads_added")
        s_acc = sem("expert_weights"); s_yu = sem("y_up")
        s_gp = sem("gate_logits_psum"); s_gm = sem("gate_shifted"); s_ge = sem("gate_exp")
        s_mw = [sem(f"moe_w1_in{i}") for i in range(2)]
        s_mv = [sem(f"moe_w2_in{i}") for i in range(2)]
        s_w1h = sem("moe_w1_hi"); s_w1s = sem("moe_w1_split")
        s_w2h = sem("moe_w2_hi"); s_w2s = sem("moe_w2_split")
        s_xh = sem("moe_x_hi"); s_xl = sem("moe_x_split")
        s_mu = sem("moe_up_psum"); s_mg = sem("moe_gelu")
        s_gl = sem("moe_gelu_split"); s_mf = sem("moe_tile_used")
        s_md = sem("moe_down_psum"); s_ma = sem("moe_added")
        s_o = sem("out_stored")
        s_own = sem("dve_own"); s_owni = sem("dve_own_init")

        NW, NLATE = 12, 9
        NCI = 5
        STK = (16 * 7, 16 * 6)

        kcut = lambda w: w.rearrange("(k p) n -> p k n", p=P)

        block = ctx.enter_context(nc.Block())

        @block.sync
        def _(sp):
            for dst, src in (
                (ident[:], a["c_ident"]), (st_dist, a["c_dist"]), (par[:], a["c_par"]), (st_kb, a["c_kb"]), (st_qb, a["c_qb"]),
            ):
                sp.dma_start(dst, src).then_inc(s_ci, 16)
            row = lambda v: v.rearrange("(a n) -> a n", a=1).broadcast_to([P, D])
            n = 0
            for dst, src in (
                (wq[0][:], kcut(a["wq0"])), (wk[0][:], kcut(a["wk0"])), (wv[0][:], kcut(a["wv0"])),
                (bqk[:, 0, :], a["bq"]), (bqk[:, 1, :], a["bk"]),
                (bv_bc[:], row(a["bv"])), (bo_bc[:], row(a["bo"])),
                (st_wq, a["w_ret"].rearrange("(a n) d -> n a d", n=RD)), (st_keys, a["keys"].rearrange("n h p k -> n (h p k)")),
                (gw[:], kcut(a["gate"])), (gcol[:, 0:KC], a["gamma"]),
                (gcol[:, KC:2 * KC], a["beta"]),
            ):
                sp.dma_start(dst, src).then_inc(s_w, 16)
                n += 1
            sp.wait_ge(s_conv, 2)
            sp.wait_ge(s_ms, 4 + SLOTS)
            for s in range(SLOTS):
                sp.dma_start(stack_k[s][BROW:MROW, :, :].bitcast(F32),
                             kb_c.bitcast(F32).unsqueeze(1).broadcast_to([NB, HG // 2, T])).then_inc(s_kbin, 16)
            assert n == NW

            with sp.Fori(0, B) as b:
                def wait(s, value):
                    sp.wait_ge(s, value)
                    sp.nop(nofuse=True)

                sp.dma_start(x_in[:], a["x"][b].rearrange("(t p) d -> p t d", p=P)).then_inc(s_x, 16)
                sp.dma_start(ctx_in[:], a["ctx"][b].rearrange("(t p) d -> p t d", p=P)).then_inc(s_ctx, 16)

                def load_k(L, g):
                    n = NG * L + g
                    s = n % SLOTS
                    if n >= SLOTS:
                        wait(s_st, b * 64 + 8 * (n - SLOTS) + 8)
                    if g % 2 == 0:
                        wait(s_ksplit, b * 4 + 2 * L + g // 2 + 1)
                    sp.dma_start(stack_q[s][BROW:MROW, :, :].bitcast(F32),
                                 qb_c[:, L, :].bitcast(F32).unsqueeze(1).broadcast_to([NB, HG, T])).then_inc(s_stk[s][0], 16)
                    for pair in range(HG // 2):
                        r, m = PR * (2 * (g % 2) + pair), g // 2
                        for blk, i in ((0, 0), (1, 0), (2, 1)):
                            sp.dma_start(stack_k[s][PR * blk:PR * (blk + 1), pair, :].bitcast(F32),
                                         ks[r:r + PR, i, m, :].bitcast(F32)).then_inc(s_stk[s][pair], 16)

                def load_q(L, g):
                    s = (NG * L + g) % SLOTS
                    if g % 2 == 0:
                        wait(s_qsplit, b * 4 + 2 * L + g // 2 + 1)
                    for pair in range(HG // 2):
                        r, m = PR * (2 * (g % 2) + pair), g // 2
                        for blk, i in ((0, 0), (1, 1), (2, 0)):
                            sp.dma_start(stack_q[s][PR * blk:PR * (blk + 1), 2 * pair:2 * pair + 2, :].bitcast(F32),
                                         qs[r:r + PR, i, m, :, :].bitcast(F32)).then_inc(s_stk[s][pair], 16)

                def load_max(L, g):
                    n = NG * L + g
                    wait(s_mc, b * 8 + n + 1)
                    sp.dma_start(stack_q[n % SLOTS][MROW:MROW + 1, :, :].bitcast(F32),
                                 m_sb[:, n % 2, :].bitcast(F32)).then_inc(s_mr[n % 2], 16)

                for L in range(2):
                    for what, g in ((load_k, 0), (load_q, 0), (load_k, 1), (load_q, 1), (load_max, 0), (load_k, 2), (load_q, 2),
                                    (load_max, 1), (load_k, 3), (load_q, 3), (load_max, 2), (load_max, 3)):
                        what(L, g)
                for e in range(ME):
                    s = e % 2
                    if e >= 2:
                        wait(s_w1s, b * ME + e - 1)
                    sp.dma_start(w1b[s], a["w1"][e].rearrange("(k p) f -> p k f", p=P)).then_inc(s_mw[s], 16)
                    if e >= 2:
                        wait(s_w2s, b * ME + e - 1)
                    sp.dma_start(w2b[s], a["w2"][e].rearrange("(k p) f -> p k f", p=P)).then_inc(s_mv[s], 16)
                wait(s_yu, b * 8 + 8)

        @block.gpsimd
        def _(pool):
            fills = [(ones[:], 1.0), (eps[:], EPS), (v_aug[:], 0.0), (v_aug[:, :, :, DH:DH + 1], 1.0)]
            for s in range(SLOTS):
                fills += [(stack_k[s][96:MROW + 1, :, :].bitcast(F32), 1.0)]
            for i, (dst, value) in enumerate(fills):
                if i:
                    pool.wait_ge(s_ms, i)
                pool.memset(dst, value).then_inc(s_ms, 1)
            pool.wait_ge(s_ms, 4 + SLOTS)
            pool.wait_ge(s_selin, 16)
            pool.tensor_copy(sel[:].rearrange("p c i m -> p (c i m)"), st_sel).then_inc(s_sel, 1)
            with pool.Fori(0, B) as b:
                pool.wait_ge(s_w, 16 * NW)
                pool.wait_ge(s_ln, b * 16 + 4)
                pool.tensor_tensor(x_in[:], x_in[:], bo_bc[:].unsqueeze(1).broadcast_to([P, TT, D]), ALU.add).then_inc(s_xb, 1)
                for i, (hi, lo, whole) in enumerate(((ff1s[0], ff1s[1], wff1), (xs[:, 0], xs[:, 1], xnT), (downs[0], downs[1], wdown_e))):
                    pool.wait_ge(s_fh, b * 3 + i + 1)
                    pool.tensor_tensor(lo, whole[:], hi.bitcast(F32), ALU.subtract).then_inc(s_fl, 1)
                    pool.wait_ge(s_fl, b * 3 + i + 1)
                for q in range(EC * RH + 1):
                    c, h = divmod(q, RH)
                    if q < EC * RH:
                        pool.wait_ge(s_pm, b * 32 + q + 1)
                        if h == 0:
                            pool.wait_ge(s_hdc, b * 8 + c + 1)
                        if q >= RING:
                            pool.wait_ge(s_g, b * 32 + q - RING + 1)
                        pool.tensor_tensor(pv_b[q % RING], pexp[q % RING], hdT[:, c % 2, :], ALU.mult).then_inc(s_u, 1)
                    if h == 0 and c:
                        pool.wait_ge(s_g, b * 32 + q - 2)
                        pool.tensor_tensor(acc[:, (c - 1) % 2, :], acc[:, (c - 1) % 2, :], wt[:, 1, :], ALU.add).then_inc(s_a01, 1)
                pool.wait_ge(s_u, b * 32 + 32)

                def split_w1(e):
                    i = e % 2
                    if e == 0:
                        pool.wait_ge(s_mw[i], b * 64 + 16)
                        pool.wait_ge(s_red, b * 128 + 128)
                        pool.nop(nofuse=True)
                        pool.tensor_copy(w1s[i][:, 0], w1b[i]).then_inc(s_w1h, 1)
                    elif e >= 2:
                        pool.wait_ge(s_w2s, b * ME + e - 1)
                    else:
                        pool.wait_ge(s_w1s, b * ME + 1)
                    pool.wait_ge(s_w1h, b * ME + e + 1)
                    pool.tensor_tensor(w1s[i][:, 1], w1b[i], w1s[i][:, 0].bitcast(F32), ALU.subtract).then_inc(s_w1s, 1)

                split_w1(0)
                for e in range(ME):
                    if e + 1 < ME:
                        split_w1(e + 1)
                        pool.wait_ge(s_w1s, b * ME + e + 2)
                    else:
                        pool.wait_ge(s_w2s, b * ME + e)
                    pool.wait_ge(s_w2h, b * ME + e + 1)
                    pool.tensor_tensor(w2s[e % 2][:, 1], w2b[e % 2], w2s[e % 2][:, 0].bitcast(F32), ALU.subtract).then_inc(s_w2s, 1)
                pool.wait_ge(s_w2s, b * ME + ME)
                pool.wait_ge(s_ma, b * 32 + 32)
                pool.dma_start(out[b].rearrange("(t p) d -> p t d", p=P), x_tok[:]).then_inc(s_o, 16)
                pool.wait_ge(s_o, b * 16 + 16)

        @block.scalar
        def _(act):
            act.wait_ge(s_w, 16 * NW)
            for dst, src in (
                (wo[:], kcut(a["wo0"])), (wff1[:], kcut(a["ff1"])), (wff2[:], kcut(a["ff2"])),
                (wdown_e[:], kcut(a["down_e"])), (wup_e[:], kcut(a["up_e"])),
                (last_up[:], a["up_e"][NE - 1:NE, :].broadcast_to([P, D])),
                (wk[1][:], kcut(a["wk1"])), (wq[1][:], kcut(a["wq1"])), (wv[1][:], kcut(a["wv1"])),
            ):
                act.dma_start(dst, src).then_inc(s_late, 16)
            act.wait_ge(s_ms, 4 + SLOTS)
            act.wait_ge(s_wret_ps, KC)
            act.dma_start(st_sel, a["c_sel"]).then_inc(s_selin, 16)

            with act.Fori(0, B) as b:
                def sqrt(i):
                    act.wait_ge(s_lnv, b * 5 + i + 1)
                    act.activation(sd[:], mv[:, :, 1], ACT.Sqrt, bias=eps[:]).then_inc(s_lnd, 1)

                def turned(i, dst, bank):
                    act.wait_ge(s_tr, b * 6 + i + 1)
                    act.copy(dst, ps[:, bank, :]).then_inc(s_tra, 1)

                def to_float(L, which):
                    for m in range(KC):
                        act.wait_ge(s_qk, b * 8 + 4 * L + 2 * (1 - which) + m + 1)
                        dst = (qf, kf)[which][:, m, :]
                        scale = (SCALE * (UNITS, 1)[L], 1.0)[which]
                        if L == 0:
                            act.activation(dst, ps[:, 2 * which + m, :], ACT.Identity, bias=bqk[:, which, m:m + 1], scale=scale).then_inc(s_qkf, 1)
                        else:
                            act.activation(dst, ps[:, 2 * which + m, :], ACT.Relu, scale=scale).then_inc(s_qkf, 1)

                def attend(L):
                    for u in range(-LEAD, NU + 1):
                        v = u + LEAD
                        if 0 <= u < NU:
                            if u >= 2:
                                act.wait_ge(s_pv, b * 32 + NU * L + u - 1)
                            for half in range(2):
                                act.wait_ge(s_st, b * 64 + 2 * (NU * L + u) + half + 1)
                                act.activation(pt[:, 4 * (u % 2) + 2 * half:4 * (u % 2) + 2 * half + 2, :],
                                               ps[:, 2 + 2 * half:4 + 2 * half, :], ACT.Exp, scale=(BIAS, 1.0)[L]).then_inc(s_e, 1)
                        if v > 0 and v % 4 == 0 and v <= NU:
                            n = NG * L + v // 4 - 1
                            act.wait_ge(s_mt, b * 8 + n + 1)
                            if n >= 2:
                                act.wait_ge(s_mr[n % 2], b * 64 + 16 * (n // 2))
                            act.copy(m_sb[:, n % 2, :], ps[0:HG * TT, 7, 0:P]).then_inc(s_mc, 1)
                        if u > 0 and u % 4 == 0:
                            n = NG * L + u // 4 - 1
                            act.wait_ge(s_pv, b * 32 + 4 * n + 4)
                            if n >= 1:
                                act.wait_ge(s_ot, b * 8 + n)
                            act.copy(oT[:], ps[:, 6, :]).then_inc(s_oT, 1)

                turned(0, ctxT[:, 0, :], 2)
                sqrt(0)
                act.wait_ge(s_conv, 3)
                to_float(0, 1)
                turned(1, xnT[:, 0, :], 0)
                to_float(0, 0)
                attend(0)
                turned(2, xnT[:, 0, :], 0)
                act.wait_ge(s_late, 16 * NLATE)
                act.copy(ff1s[0], wff1[:]).then_inc(s_fh, 1)
                sqrt(1)
                turned(3, xnT[:, 0, :], 0)
                act.wait_ge(s_trd, b * 6 + 4)
                act.wait_ge(s_tra, b * 6 + 4)
                act.copy(xs[:, 0], xnT[:]).then_inc(s_fh, 1)
                for t in range(TT):
                    act.wait_ge(s_v, b * 8 + 4 + t + 1)
                    act.activation(v_aug[:, t, :, 0:DH], v_psum(1, t).rearrange("p (h c) -> p h c", c=DH),
                                   ACT.Relu).then_inc(s_va, 1)
                for t in range(TT):
                    act.wait_ge(s_sim, b * 4 + t + 1)
                    act.copy(simcat[:, t, :, :].rearrange("p h c -> p (h c)"), ps[:, 2 + t, :]).then_inc(s_simc, 1)
                act.wait_ge(s_hc, b + 1)
                act.copy(hdc[:], ps[:, 6, 0:TT]).then_inc(s_hcc, 1)
                for f in range(FC):
                    act.wait_ge(s_f, b * 8 + f + 1)
                    if f >= 2:
                        act.wait_ge(s_fd, b * 8 + f - 1)
                    act.activation(ffh[:, f % 2, :], ps[:, f % 2, :], ACT.Silu).then_inc(s_fs, 1)
                    if f == 1:
                        act.copy(downs[0], wdown_e[:]).then_inc(s_fh, 1)
                act.wait_ge(s_d8, b + 1)
                act.activation(e8[:], v8[:], ACT.Exp).then_inc(s_e8, 1)
                act.wait_ge(s_z8, b + 1)
                act.activation(lnz[:], zz[:], ACT.Ln).then_inc(s_l8, 1)
                act.activation(scratch[:], eps[:], ACT.Exp)
                for h in range(RH):
                    act.wait_ge(s_tt, b * 4 + h + 1)
                    act.copy(tr[:, 2 * h, :], ps[0:TROWS, TBANK[h], :]).then_inc(s_th, 1)
                for q in range(EC * RH + 2):
                    c, h = divmod(q, RH)
                    if q < EC * RH:
                        if h == 0:
                            act.wait_ge(s_hd, b * 8 + c + 1)
                            if c >= 2:
                                act.wait_ge(s_u, b * 32 + RH * (c - 1))
                            act.activation(hdT[:, c % 2, :], ps[:, c % 2, :], ACT.Copy, scale=0.5).then_inc(s_hdc, 1)
                        act.wait_ge(s_l, b * 32 + q + 1)
                        if q >= RING:
                            act.wait_ge(s_u, b * 32 + q - RING + 1)
                        act.activation(pexp[q % RING], ps[:, 2 + q % 2, :], ACT.Exp).then_inc(s_pe, 1)
                    if q >= 2:
                        act.wait_ge(s_u, b * 32 + q - 1)
                        if q >= 4:
                            act.wait_ge(s_g, b * 32 + q - 3)
                        act.activation(pth[q % 2], pv_b[(q - 2) % RING], ACT.Tanh).then_inc(s_t, 1)
                    if q == 10:
                        act.wait_ge(s_a64, b + 1)
                        act.activation(e64, e64, ACT.Exp).then_inc(s_x64, 1)
                act.wait_ge(s_c64, b + 1)
                for t in range(TT):
                    cols = e64[:, RH * t:RH * (t + 1), :]
                    act.activation(cols, cols, ACT.Silu, scale=hdc[:, t:t + 1], accum_out=wc[:, t:t + 1]).then_inc(s_wc, 1)
                sqrt(2)
                to_float(1, 1)
                turned(4, xnT[:, 0, :], 0)
                to_float(1, 0)
                attend(1)
                def w1_hi(e):
                    act.wait_ge(s_mw[e % 2], b * 64 + 16 * (e // 2 + 1))
                    if e == 1:
                        act.wait_ge(s_st, b * 64 + 64)
                    act.copy(w1s[e % 2][:, 0], w1b[e % 2]).then_inc(s_w1h, 1)

                def w2_hi(e):
                    act.wait_ge(s_mv[e % 2], b * 64 + 16 * (e // 2 + 1))
                    act.copy(w2s[e % 2][:, 0], w2b[e % 2]).then_inc(s_w2h, 1)

                act.wait_ge(s_w1h, b * ME + 1)
                w1_hi(1)
                w2_hi(0)
                sqrt(3)
                act.wait_ge(s_tr, b * 6 + 6)
                for k in range(KC):
                    act.copy(xs[:, 0, k, :], ps[:, 4 + k, :]).then_inc(s_xh, 1)
                act.wait_ge(s_xl, b * 2 + 1)
                turned(5, xnT[:, 0, :], 4)
                sqrt(4)

                for e in range(ME):
                    for f in range(MC):
                        act.wait_ge(s_mu, b * 32 + MC * e + f + 1)
                        if MC * e + f >= 2:
                            act.wait_ge(s_gl, b * 32 + MC * e + f - 1)
                        act.activation(g_raw[:, f % 2, :], ps[:, f, :], ACT.Gelu).then_inc(s_mg, 1)
                        if f == 0 and 2 <= e + 1 < ME:
                            w1_hi(e + 1)
                        if f == 2 and e:
                            w2_hi(e)
                    if e == 0:
                        act.wait_ge(s_gm, b + 1)
                        act.activation(ee[:], lg2[:], ACT.Exp).then_inc(s_ge, 1)

        @block.tensor
        def _(pe):
            def turn(bank, src, rows=P):
                for k in range(KC):
                    for t in range(TT):
                        ins = pe.transpose(ps[:, bank + k, t * P:(t + 1) * P], src[:, t, k * P:(k + 1) * P], ident[:])
                return ins

            pe.wait_ge(s_w, 16 * NW)
            pe.wait_ge(s_ci, 16 * NCI)
            pe.wait_ge(s_ms, 1)
            for k in range(KC):
                for h in range(RH):
                    for half in range(2):
                        p = 1 - half
                        ins = pe.matmul(ps[:, k, (2 * h + half) * NK:(2 * h + half + 1) * NK],
                                        st_wq[:, RH * p + h, k * P:(k + 1) * P],
                                        st_keys[:, (2 * h + p) * NK:(2 * h + p + 1) * NK], start=True, stop=True)
                ins.then_inc(s_wret_ps, 1)
            pe.wait_ge(s_gi, 1)
            for i, src in enumerate((gw[:], lg[:, 0:KC, :])):
                for k in range(KC):
                    ins = pe.matmul(ps[:, 2 + i, 0:ME], ones[:], src[:, k, :], start=(k == 0), stop=(k == KC - 1))
            ins.then_inc(s_wret_ps, 1)
            pe.wait_ge(s_ms, 4 + SLOTS)
            pe.wait_ge(s_kbin, 16 * SLOTS)
            pe.wait_ge(s_conv, 3)
            pe.wait_ge(s_wret, 1)

            with pe.Fori(0, B) as b:
                def turned(i):
                    pe.wait_ge(s_tra, b * 6 + i + 1)
                    pe.wait_ge(s_trd, b * 6 + i + 1)

                def products(dst, lhs, rhs, first, last):
                    for i, j in ((0, 0), (0, 1), (1, 0)):
                        ins = pe.matmul(dst, lhs(i), rhs(j), start=(first and i == j == 0), stop=(last and i == 1))
                    return ins

                def turn_norm(i, bank):
                    for t in range(TT):
                        pe.wait_ge(s_ln, b * 16 + TT * i + t + 1)
                        for k in range(KC):
                            ins = pe.transpose(ps[:, bank + k, t * P:(t + 1) * P], xn[:, t, k * P:(k + 1) * P], ident[:])
                    ins.then_inc(s_tr, 1)

                def project(L, which, chunks=range(KC)):
                    w, src = (wq, wk)[which][L], (xnT, ctxT)[which]
                    for m in chunks:
                        for k in range(KC):
                            if (L, which, m, k) == (1, 1, 1, 1):
                                pe.wait_ge(s_lnv, b * 5 + 3)
                            ins = pe.matmul(ps[:, 2 * which + m, :], w[:, k, m * P:(m + 1) * P], src[:, k, :], start=(k == 0), stop=(k == KC - 1))
                        ins.then_inc(s_qk, 1)

                def project_v(L):
                    for t in range(TT):
                        for k in range(KC):
                            ins = pe.matmul(v_psum(L, t), ctxT[:, k, t * P:(t + 1) * P], wv[L][:, k, :], start=(k == 0), stop=(k == KC - 1))
                        ins.then_inc(s_v, 1)

                def scores_by_key(L, u, half):
                    g, c = divmod(u, TT)
                    n = NG * L + g
                    s = n % SLOTS
                    if u == 0 and half == 0:
                        pe.wait_ge(s_va, b * 8 + 4 * L + 4)
                        pe.wait_ge(s_red, b * 128 + 64 * L + 4 * LEAD)
                    if c == 0 and half == 0:
                        pe.wait_ge(s_mr[n % 2], b * 64 + 16 * (n // 2 + 1))
                    if u:
                        pe.wait_ge(s_e, b * 64 + 2 * (NU * L + u - 1) + half + 1)
                    for j in (2 * half, 2 * half + 1):
                        ins = pe.matmul(ps[:, 2 + j, :], stack_k[s][0:MROW + 1, j // 2, c * P:(c + 1) * P],
                                        stack_q[s][0:MROW + 1, j, :], start=True, stop=(L == 1))
                        if L == 0:
                            ins = pe.matmul(ps[:, 2 + j, c * P:(c + 1) * P], neg16[:], dist16[:], start=False, stop=True)
                    ins.then_inc(s_st, 1)

                def scores_by_query(L, v, t):
                    g, j = divmod(v, HG)
                    n = NG * L + g
                    s = n % SLOTS
                    if j % 2 == 0 and t == 0:
                        per, before = slot_turn(n)
                        pe.wait_ge(s_stk[s][j // 2], b * (per * STK[j // 2]) + (before + 1) * STK[j // 2])
                    banks = max_banks(v)
                    if v:
                        pe.wait_ge(s_red, b * 128 + 64 * L + 4 * v + t + 1 - banks)
                    elif t == 1:
                        pe.wait_ge(s_qkf, b * 8 + 4 * L + 4)
                    pe.matmul(ps[:, t % banks, :], stack_q[s][0:MROW, j, t * P:(t + 1) * P],
                              stack_k[s][0:MROW, j // 2, :], start=True, stop=True).then_inc(s_s, 1)

                def values(L, u):
                    g, c = divmod(u, TT)
                    n = NG * L + g
                    pe.wait_ge(s_e, b * 64 + 2 * (NU * L + u) + 2)
                    if c == 0 and n:
                        pe.wait_ge(s_oT, b * 8 + n)
                    for j in range(HG):
                        ins = pe.matmul(ps[32 * j:32 * j + 32, 6, :], v_aug[:, c, HG * g + j, :],
                                        pt[:, 4 * (u % 2) + j, :], start=(c == 0), stop=(c == TT - 1))
                    ins.then_inc(s_pv, 1)

                def attend(L):
                    for u in range(-LEAD, NU + 2):
                        v = u + LEAD
                        for what, t in ORDER:
                            if what == "key" and 0 <= u < NU:
                                scores_by_key(L, u, t)
                            if what == "values" and 1 <= u <= NU:
                                values(L, u - 1)
                            if what == "query" and v < NU:
                                scores_by_query(L, v, t)
                        if v > 0 and v % 4 == 0 and v <= NU:
                            n = NG * L + v // 4 - 1
                            pe.wait_ge(s_red, b * 128 + 16 * (n + 1))
                            if n == NG * L:
                                pe.wait_ge(s_va, b * 8 + 4 * L + 4)
                            if n - NG * L >= 2:
                                pe.wait_ge(s_on, b * 8 + n - 1)
                            pe.transpose(ps[0:HG * TT, 7, 0:P], negmax[:, n % 2, :], ident[:]).then_inc(s_mt, 1)
                        if u >= 5 and u % 4 == 1:
                            n = NG * L + (u - 5) // 4
                            pe.wait_ge(s_oT, b * 8 + n + 1)
                            if n >= 1:
                                pe.wait_ge(s_on, b * 8 + n)
                            pe.wait_ge(s_mc, b * 8 + min(NG * L + NG, n + 2))
                            for t in range(TT):
                                ins = pe.transpose(ps[:, 7, t * P:(t + 1) * P], oT[:, t * P:(t + 1) * P], ident[:])
                            ins.then_inc(s_ot, 1)

                pe.wait_ge(s_ctx, b * 16 + 16)
                turn(2, ctx_in).then_inc(s_tr, 1)
                turned(0)
                project(0, 1)
                turn_norm(0, 0)
                turned(1)
                project(0, 0)
                project_v(0)
                attend(0)
                pe.wait_ge(s_on, b * 8 + 4)
                turn(0, xn).then_inc(s_tr, 1)
                turned(2)
                pe.wait_ge(s_late, 16 * NLATE)
                for t in range(TT):
                    for k in range(KC):
                        ins = pe.matmul(ps[:, 2 + t, 0:D], xnT[:, k, t * P:(t + 1) * P], wo[:, k, :], start=(k == 0), stop=(k == KC - 1))
                    ins.then_inc(s_wo, 1)
                project_v(1)
                turn_norm(1, 0)
                turned(3)
                for t in range(TT):
                    for k in range(KC):
                        ins = pe.matmul(ps[:, 2 + t, :], xnT[:, k, t * P:(t + 1) * P], wret[:, k, :], start=(k == 0), stop=(k == KC - 1))
                    ins.then_inc(s_sim, 1)
                for t in range(TT):
                    for k in range(KC):
                        if t == 0 and k == 0:
                            pe.wait_ge(s_va, b * 8 + 8)
                        ins = pe.matmul(ps[:, 6, t:t + 1], xnT[:, k, t * P:(t + 1) * P], wdown_e[:, k, NE - 1:NE], start=(k == 0), stop=(k == KC - 1))
                ins.then_inc(s_hc, 1)
                def add_y(lhs, rhs, first, tiles=range(TT)):
                    for t in tiles:
                        ins = pe.matmul(ps[:, 6 + t // 2, (t % 2) * D:(t % 2 + 1) * D], lhs[:, t * P:(t + 1) * P], rhs,
                                        start=(first and t % 2 == 0), stop=True, skip_group_check=True)
                    return ins

                for f in range(FC + 1):
                    if f < FC:
                        if f >= 2:
                            pe.wait_ge(s_fs, b * 8 + f - 1)
                        if f == 0:
                            pe.wait_ge(s_fl, b * 3 + 2)
                        for k in range(KC):
                            ins = products(ps[:, f % 2, :], lambda i: ff1s[i][:, k, f * P:(f + 1) * P], lambda j: xs[:, j, k, :], k == 0, k == KC - 1)
                        ins.then_inc(s_f, 1)
                    if f >= 1:
                        if f == 1:
                            pe.wait_ge(s_hcc, b + 1)
                        pe.wait_ge(s_fs, b * 8 + f)
                        add_y(ffh[:, (f - 1) % 2, :], wff2[:, f - 1, :], f == 1).then_inc(s_fd, 1)
                def expert_products(c, k):
                    if c >= 2 and k == 0:
                        pe.wait_ge(s_hdc, b * 8 + c - 1)
                    ins = products(ps[:, c % 2, :], lambda i: downs[i][:, k, c * P:(c + 1) * P], lambda j: xs[:, j, k, :], k == 0, k == KC - 1)
                    if k == KC - 1:
                        ins.then_inc(s_hd, 1)

                pe.wait_ge(s_fl, b * 3 + 3)
                for k in range(KC):
                    expert_products(0, k)
                pe.wait_ge(s_sel, 1)
                pe.wait_ge(s_row, b + 1)
                for h in range(RH):
                    for t in range(TT):
                        ins = pe.transpose(ps[0:TROWS, TBANK[h], t * P:(t + 1) * P], simcat[:, t, h, 0:TROWS], ident[:])
                    ins.then_inc(s_tt, 1)
                for q in range(RH * EC + 8):
                    c, h = divmod(q, RH)
                    if q == RH * EC + 1:
                        pe.wait_ge(s_t, b * 32 + 30)
                        project(1, 1, (0,))
                    if q < 2:
                        pe.wait_ge(s_th, b * 4 + 2 * q + 2)
                        pe.wait_ge(s_tl, b * 4 + 2 * q + 2)
                    if q < RH * EC:
                        for i0, base, done, mine in ((0, 2, s_pe, s_l), (1, 4, s_pm, s_m)):
                            if q >= 2:
                                pe.wait_ge(done, b * 32 + q - 1)
                            for i in range(2):
                                ins = pe.matmul(ps[:, base + q % 2, :], sel[:, c, i0, :], tr[:, 2 * h + i, :], start=(i == 0), stop=(i == 1))
                            ins.then_inc(mine, 1)
                        if h % 2 == 0 and c + 1 < EC:
                            expert_products(c + 1, h // 2)
                    if c >= 2 and h:
                        if h == 1:
                            pe.wait_ge(s_acc, b * 8 + c - 1)
                        ins = add_y(acc[:, c % 2, :], wup_e[:, c - 2, :], False, ((0, 1), (2,), (3,))[h - 1])
                        if h == 3:
                            ins.then_inc(s_yu, 1)
                project(1, 1, (1,))
                turn_norm(2, 0)
                turned(4)
                project(1, 0)
                attend(1)
                turn_norm(3, 4)

                def expert_up(e, tiles=range(MC)):
                    pe.wait_ge(s_w1s, b * ME + e + 1)
                    for f in tiles:
                        if e:
                            pe.wait_ge(s_mg, b * 32 + MC * (e - 1) + f + 1)
                        for k in range(KC):
                            if e == 0 and f == 0:
                                pe.wait_ge(s_xl, b * 2 + k + 1)
                            ins = products(ps[:, f, :], lambda i: w1s[e % 2][:, i, k, f * P:(f + 1) * P], lambda j: xs[:, j, k, :],
                                           k == 0, k == KC - 1)
                        ins.then_inc(s_mu, 1)

                def expert_down(e, f):
                    pe.wait_ge(s_gl, b * 32 + MC * e + f + 1)
                    if f == 0:
                        pe.wait_ge(s_w2s, b * ME + e + 1)
                    for t in range(TT):
                        if f == 0 and e >= 1:
                            pe.wait_ge(s_ma, b * 32 + 4 * (e - 1) + t + 1)
                        elif f == 0 and t == 3:
                            pe.wait_ge(s_gm, b + 1)
                        ins = products(ps[:, 4 + t, 0:D], lambda i: gs[f][:, i, t * P:(t + 1) * P], lambda j: w2s[e % 2][:, j, f, :],
                                       f == 0, f == MC - 1)
                        if f == MC - 1:
                            ins.then_inc(s_md, 1)
                    if f < MC - 1:
                        ins.then_inc(s_mf, 1)

                expert_up(0, (0, 1))
                turned(5)
                pe.wait_ge(s_on, b * 8 + 8)
                for t in range(TT):
                    for k in range(KC):
                        ins = pe.matmul(ps[:, 7, t * ME:(t + 1) * ME], xnT[:, k, t * P:(t + 1) * P], gw[:, k, :], start=(k == 0), stop=(k == KC - 1))
                ins.then_inc(s_gp, 1)
                expert_up(0, (2, 3))
                for e in range(1, ME + 1):
                    for f in range(MC):
                        if e < ME:
                            expert_up(e, (f,))
                        expert_down(e - 1, f)

        @block.vector
        def _(dve):
            own = Own(dve, s_owni, 0, 0)
            dve.wait_ge(s_ci, 16 * NCI)
            dve.tensor_copy(kb_c, st_kb).then_inc(s_conv, 1)
            dve.tensor_copy(qb_c[:], st_qb).then_inc(s_conv, 1)
            own(dve.tensor_scalar(neg16[:], ident[:], -1.0, None, ALU.mult))
            own(dve.tensor_copy(dist16[:], st_dist))
            dve.wait_ge(s_w, 16 * NW)
            for k in range(KC):
                own(dve.tensor_scalar(lg[:, k, :], gw[:, k, :], gcol[:, KC + k:KC + k + 1], None, ALU.mult))
            dve.wait_ge(s_owni, own.k)
            for k in range(KC):
                own(dve.tensor_scalar(gw[:, k, :], gw[:, k, :], gcol[:, k:k + 1], None, ALU.mult))
            dve.wait_ge(s_owni, own.k)
            dve.tensor_scalar(bqk[:, 0, :], bqk[:, 0, :], SCALE * UNITS, None, ALU.mult).then_inc(s_conv, 1)
            dve.wait_ge(s_conv, 3)
            dve.sem_inc(s_gi, 1)
            for k in range(KC):
                dve.wait_ge(s_wret_ps, k + 1)
                own(dve.tensor_copy(wret[:, k, :], ps[:, k, :]))
            dve.wait_ge(s_wret_ps, KC + 1)
            for i in range(2):
                own(dve.tensor_copy(gbc[:, i, :], ps[:, 2 + i, 0:ME]))
            dve.wait_ge(s_owni, own.k)
            dve.sem_inc(s_wret, 1)

            with dve.Fori(0, B) as b:
                own = Own(dve, s_own, OWN_STEPS, b)

                def stats(i, src):
                    for t in range(TT):
                        own(dve.bn_stats(st6[:, t, :], src[:, t, :]))
                    own.wait(alone=True)
                    for t in range(TT):
                        ins = dve.bn_aggr(mv[:, t, :], st6[:, t, :])
                    ins.then_inc(s_lnv, 1)
                    dve.wait_ge(s_lnd, b * 5 + i + 1)
                    own(dve.reciprocal(rstd[:], sd[:]))
                    own.wait()

                def layernorm(i, src):
                    stats(i, src)
                    for t in range(TT):
                        dve.tensor_scalar(xn[:, t, :], src[:, t, :], mv[:, t, 0:1], rstd[:, t:t + 1], ALU.subtract, ALU.mult).then_inc(s_ln, 1)

                def turned(i, dst, bank):
                    dve.wait_ge(s_tr, b * 6 + i + 1)
                    dve.tensor_copy(dst, ps[:, bank, :]).then_inc(s_trd, 1)

                def split_qk(L):
                    for m in range(KC):
                        dve.wait_ge(s_qkf, b * 8 + 4 * L + m + 1)
                        own(dve.tensor_copy(ks[:, 0, m, :], kf[:, m, :]))
                        own.wait()
                        dve.tensor_tensor(ks[:, 1, m, :], kf[:, m, :], ks[:, 0, m, :].bitcast(F32), ALU.subtract).then_inc(s_ksplit, 1)
                    for m in range(KC):
                        dve.wait_ge(s_qkf, b * 8 + 4 * L + 2 + m + 1)
                        for h in range(2):
                            own(dve.tensor_scalar(qs[:, 0, m, h, :], qf[:, m, :], par[:, h:h + 1], None, ALU.mult))
                        own.wait()
                        for h in range(2):
                            ins = dve.scalar_tensor_tensor(out=qs[:, 1, m, h, :], in0=qf[:, m, :], scalar=par[:, h:h + 1],
                                                           in1=qs[:, 0, m, h, :].bitcast(F32), op0=ALU.mult, op1=ALU.subtract)
                        ins.then_inc(s_qsplit, 1)

                def attend(L):
                    for u in range(-LEAD, NU + 2):
                        v = u + LEAD
                        if 0 <= v < NU:
                            g, j = divmod(v, HG)
                            n = NG * L + g
                            if j == 0 and n >= 2:
                                dve.wait_ge(s_mt, b * 8 + n - 1)
                            for t in range(TT):
                                dve.wait_ge(s_s, b * 128 + 64 * L + 4 * v + t + 1)
                                dve.tensor_reduce(negmax[:, n % 2, 4 * j + t:4 * j + t + 1], ps[:, t % max_banks(v), :], AX, ALU.max, negate=True).then_inc(s_red, 1)
                        if u >= 5 and u % 4 == 1:
                            g = (u - 5) // 4
                            n = NG * L + g
                            dve.wait_ge(s_ot, b * 8 + n + 1)
                            o4 = ps[:, 7, :].rearrange("p (t j c) -> p t j c", t=TT, j=HG)
                            own(dve.reciprocal(rec[:], o4[:, :, :, DH]))
                            own.wait()
                            dst = xn[:, :, 64 * g:64 * (g + 1)].rearrange("p t (j c) -> p t j c", c=DH)
                            dve.tensor_tensor(dst, o4[:, :, :, 0:DH], rec[:].unsqueeze(3).broadcast_to([P, TT, HG, DH]), ALU.mult).then_inc(s_on, 1)
                            if L == 1:
                                dve.wait_ge(s_on, b * 8 + n + 1)
                                cols = slice(64 * g, 64 * (g + 1))
                                own(dve.tensor_tensor(x_tok[:, :, cols], x_tok[:, :, cols], xn[:, :, cols], ALU.add))

                dve.wait_ge(s_x, b * 16 + 16)
                turned(0, ctxT[:, 1, :], 3)
                layernorm(0, x_in)
                turned(1, xnT[:, 1, :], 1)
                split_qk(0)
                dve.wait_ge(s_ms, 4 + SLOTS)
                for t in range(TT):
                    dve.wait_ge(s_v, b * 8 + t + 1)
                    dve.tensor_tensor(v_aug[:, t, :, 0:DH], ps[:, 4 + t, 0:D].rearrange("p (h c) -> p h c", c=DH),
                                      bv_bc[:].rearrange("p (h c) -> p h c", c=DH), ALU.add).then_inc(s_va, 1)
                attend(0)
                turned(2, xnT[:, 1, :], 1)
                dve.wait_ge(s_xb, b + 1)
                for t in range(TT):
                    dve.wait_ge(s_wo, b * 4 + t + 1)
                    dve.tensor_tensor(x_tok[:, t, :], ps[:, 2 + t, 0:D], x_in[:, t, :], ALU.add).then_inc(s_x1, 1)
                dve.wait_ge(s_x1, b * 4 + 4)
                layernorm(1, x_tok)
                turned(3, xnT[:, 1, :], 1)
                for t in range(TT):
                    dve.wait_ge(s_simc, b * 4 + t + 1)
                    dve.nop(nofuse=True)
                    for h in range(RH):
                        own(dve.max(sy8[:, RH * t + h, :], simcat[:, t, h, 0:NK]))
                        own(dve.max(sx8[:, RH * t + h, :], simcat[:, t, h, NK:2 * NK]))
                own.wait(alone=True)
                for t in range(TT):
                    for h in range(RH):
                        own(dve.max_index(ix8[:, RH * t + h, :], sx8[:, RH * t + h, :], simcat[:, t, h, NK:2 * NK]))
                R = TT * RH
                own(dve.tensor_tensor(s64.rearrange("p a (i j) -> p a i j", j=8), sx8[:].unsqueeze(3).broadcast_to([P, R, 8, 8]),
                                      sy8[:].unsqueeze(2).broadcast_to([P, R, 8, 8]), ALU.add))
                own(dve.tensor_reduce(mag[:, 0, :], sx8[:], AX, ALU.add, apply_absolute_value=True))
                own(dve.tensor_reduce(mag[:, 1, :], sy8[:], AX, ALU.add, apply_absolute_value=True))
                own.wait()
                own(dve.tensor_scalar(ixg[:], ix8[:], float(NX), None, ALU.is_ge))
                own(dve.tensor_tensor(mag[:, 0, :], mag[:, 0, :], mag[:, 1, :], ALU.add))
                for r in range(R):
                    own(dve.max(v8[:, r, :], s64[:, r, :]))
                own.wait()
                own(dve.tensor_tensor(c64[:], s64, v8[:, :, 7:8].broadcast_to([P, R, 64]), ALU.is_ge))
                own(dve.scalar_tensor_tensor(out=simcat.rearrange("p t h c -> p (t h) c")[:, :, R_THR], in0=mag[:, 0, :], scalar=DELTA,
                                             in1=v8[:, :, 7], op0=ALU.mult, op1=ALU.subtract))
                own(dve.tensor_copy(zz[:], v8[:, :, 0]))
                own.wait()
                dve.tensor_tensor(v8[:], v8[:], zz[:].unsqueeze(2).broadcast_to([P, R, 8]), ALU.subtract).then_inc(s_d8, 1)
                own(dve.tensor_tensor(c64[:].rearrange("p a (i j) -> p (a i) j", j=8), c64[:].rearrange("p a (i j) -> p (a i) j", j=8),
                                      ixg[:].rearrange("p a i -> p (a i)").unsqueeze(2).broadcast_to([P, R * 8, 8]), ALU.mult))
                own(dve.tensor_copy(mag[:, 1, :], zz[:]))
                own.wait()
                dve.wait_ge(s_e8, b + 1)
                dve.tensor_reduce(zz[:], e8[:], AX, ALU.add).then_inc(s_z8, 1)
                dve.wait_ge(s_l8, b + 1)
                dve.scalar_tensor_tensor(out=simcat.rearrange("p t h c -> p (t h) c")[:, :, R_LOGIT], in0=lnz[:], scalar=-1.0,
                                         in1=mag[:, 1, :], op0=ALU.mult, op1=ALU.subtract).then_inc(s_row, 1)
                dve.wait_ge(s_row, b + 1)
                for h in range(RH):
                    dve.wait_ge(s_th, b * 4 + h + 1)
                    dve.tensor_tensor(tr[:, 2 * h + 1, :], ps[0:TROWS, TBANK[h], :], tr[:, 2 * h, :].bitcast(F32), ALU.subtract).then_inc(s_tl, 1)
                for q in range(EC * RH + 4):
                    if q < EC * RH:
                        dve.wait_ge(s_m, b * 32 + q + 1)
                        dve.wait_ge(s_pe, b * 32 + q + 1)
                        dve.scalar_tensor_tensor(out=pexp[q % RING], in0=ps[:, 4 + q % 2, :], scalar=0.0, in1=pexp[q % RING],
                                                 op0=ALU.is_ge, op1=ALU.mult).then_inc(s_pm, 1)
                    if 3 <= q < EC * RH + 3:
                        c, h = divmod(q - 3, RH)
                        dve.wait_ge(s_t, b * 32 + q - 2)
                        if h == 0 and c >= 2:
                            dve.wait_ge(s_yu, b * 8 + c - 1)
                        if h == 1 and c:
                            dve.wait_ge(s_acc, b * 8 + c)
                        if h == 3:
                            dve.wait_ge(s_a01, b * 8 + c + 1)
                        dve.scalar_tensor_tensor(out=acc[:, c % 2, :] if h == 0 else wt[:, h % 2, :], in0=pth[(q - 3) % 2], scalar=1.0,
                                                 in1=pv_b[(q - 3) % RING], op0=ALU.add, op1=ALU.mult).then_inc(s_g, 1)
                    if q == 8:
                        dve.tensor_tensor(e64, s64, simcat.rearrange("p t h c -> p (t h) c")[:, :, R_LOGIT:R_LOGIT + 1].broadcast_to([P, R, 64]),
                                          ALU.add).then_inc(s_a64, 1)
                    if q == 16:
                        dve.wait_ge(s_x64, b + 1)
                        dve.tensor_tensor(e64, e64, c64[:], ALU.mult).then_inc(s_c64, 1)
                    if q >= 4:
                        c, h = divmod(q - 4, RH)
                        if h >= 2:
                            dve.wait_ge(s_g, b * 32 + q - 3)
                        if h == 2:
                            dve.wait_ge(s_a01, b * 8 + c + 1)
                            own(dve.tensor_tensor(acc[:, c % 2, :], acc[:, c % 2, :], wt[:, 0, :], ALU.add))
                        if h == 3:
                            own.wait()
                            dve.tensor_tensor(acc[:, c % 2, :], acc[:, c % 2, :], wt[:, 1, :], ALU.add).then_inc(s_acc, 1)
                dve.wait_ge(s_wc, b * 4 + 4)
                for t in range(TT):
                    own(dve.scalar_tensor_tensor(out=x_tok[:, t, :], in0=last_up[:], scalar=wc[:, t:t + 1], in1=x_tok[:, t, :],
                                                 op0=ALU.mult, op1=ALU.add))
                own.wait()
                dve.wait_ge(s_yu, b * 8 + 8)
                for i in range(2):
                    own(dve.tensor_tensor(x_tok[:, 2 * i:2 * i + 2, :].rearrange("p t d -> p (t d)"), ps[:, 6 + i, :],
                                          x_tok[:, 2 * i:2 * i + 2, :].rearrange("p t d -> p (t d)"), ALU.add))
                own.wait()
                layernorm(2, x_tok)
                turned(4, xnT[:, 1, :], 1)
                split_qk(1)
                attend(1)
                own.wait()
                layernorm(3, x_tok)
                for k in range(KC):
                    dve.wait_ge(s_xh, b * 2 + k + 1)
                    dve.tensor_tensor(xs[:, 1, k, :], ps[:, 4 + k, :], xs[:, 0, k, :].bitcast(F32), ALU.subtract).then_inc(s_xl, 1)
                turned(5, xnT[:, 1, :], 5)
                dve.wait_ge(s_ln, b * 16 + 16)
                stats(4, xn)
                own(dve.tensor_tensor(lg2[:], gbc[:, 0, :].unsqueeze(1).broadcast_to([P, TT, ME]), mv[:, :, 0:1].broadcast_to([P, TT, ME]), ALU.mult))
                own.wait()
                dve.wait_ge(s_gp, b + 1)
                own(dve.tensor_tensor(lg[:], ps[:, 7, 0:TT * ME].rearrange("p (t e) -> p t e", e=ME), lg2[:], ALU.subtract))
                own.wait()
                own(dve.tensor_tensor(lg[:], lg[:], rstd[:].unsqueeze(2).broadcast_to([P, TT, ME]), ALU.mult))
                own.wait()
                own(dve.tensor_tensor(lg[:], lg[:], gbc[:, 1, :].unsqueeze(1).broadcast_to([P, TT, ME]), ALU.add))
                own.wait(alone=True)
                for t in range(TT):
                    own(dve.max(mx8[:, t, :], lg[:, t, :]))
                own.wait()
                dve.tensor_tensor(lg2[:], lg[:], mx8[:, :, 0:1].broadcast_to([P, TT, ME]), ALU.subtract).then_inc(s_gm, 1)
                own(dve.tensor_tensor(comb[:], lg[:], mx8[:, :, 1:2].broadcast_to([P, TT, ME]), ALU.is_ge))

                def gate():
                    dve.wait_ge(s_ge, b + 1)
                    own(dve.tensor_reduce(gz[:], ee[:], AX, ALU.add))
                    own.wait()
                    own(dve.reciprocal(gz[:], gz[:]))
                    own(dve.tensor_tensor(comb[:], comb[:], ee[:], ALU.mult))
                    own.wait()
                    own(dve.tensor_tensor(comb[:], comb[:], gz[:].unsqueeze(2).broadcast_to([P, TT, ME]), ALU.mult))
                    own.wait()

                for e in range(ME + 1):
                    for f in range(MC):
                        if e and f == MC - 1:
                            for t in range(TT):
                                dve.wait_ge(s_md, b * 32 + 4 * (e - 1) + t + 1)
                                if e >= 2:
                                    dve.wait_ge(s_ma, b * 32 + 4 * (e - 2) + t + 1)
                                dve.scalar_tensor_tensor(out=x_tok[:, t, :], in0=ps[:, 4 + t, 0:D], scalar=comb[:, t, e - 1:e],
                                                         in1=x_tok[:, t, :], op0=ALU.mult, op1=ALU.add).then_inc(s_ma, 1)
                        if e < ME:
                            hi, lo = (gs[f][:, i, :] for i in range(2))
                            dve.wait_ge(s_mg, b * 32 + MC * e + f + 1)
                            if e and f < MC - 1:
                                dve.wait_ge(s_mf, b * 24 + (MC - 1) * (e - 1) + f + 1)
                            own(dve.tensor_copy(hi, g_raw[:, f % 2, :]))
                            own.wait()
                            dve.tensor_tensor(lo, g_raw[:, f % 2, :], hi.bitcast(F32), ALU.subtract).then_inc(s_gl, 1)
                    if e == 0:
                        gate()
                own.close()


OWN_STEPS = 182


def layout(i):
    c = np.ascontiguousarray
    f = lambda n: np.asarray(i[n])
    cols = lambda n: c(f(n).reshape(KC, P).T)
    return {
        "x": c(f("x")), "ctx": c(f("ctx_1024")),
        "wq0": c(f("L0_xattn_Wq").T), "wk0": c(f("L0_xattn_Wk").T), "wv0": c(f("L0_xattn_Wv").T), "wo0": c(f("L0_xattn_Wo").T),
        "bq": cols("L0_xattn_bq"), "bk": cols("L0_xattn_bk"), "bv": c(f("L0_xattn_bv")), "bo": c(f("L0_xattn_bo")),
        "w_ret": c(f("L0_ffn_W_q")), "keys": c(f("L0_ffn_keys").transpose(3, 0, 2, 1)),
        "down_e": c(f("L0_ffn_down_embed").T), "up_e": c(f("L0_ffn_up_embed")),
        "ff1": c(f("L0_ffn_W_up").T), "ff2": c(f("L0_ffn_W_down").T),
        "wq1": c(f("L1_xattn_Wq").T), "wk1": c(f("L1_xattn_Wk").T), "wv1": c(f("L1_xattn_Wv").T),
        "gate": c(f("L1_ffn_gate_w").T), "gamma": cols("L1_ffn_ln_gamma"), "beta": cols("L1_ffn_ln_beta"),
        "w1": c(f("L1_ffn_w1").transpose(0, 2, 1)), "w2": c(f("L1_ffn_w2").transpose(0, 2, 1)),
    }


def kernel(**inputs):
    import concourse.bacc as bacc
    from concourse.bass_utils import run_bass_kernel_spmd

    nc = bacc.Bacc("TRN2", target_bir_lowering=False, num_devices=1, dynamic_dma_scratch_size=8192)
    arrays = {**layout(inputs), **shape_constants()}
    aps = {k: nc.dram_tensor("in_" + k, v.shape, mybir.dt.from_np(v.dtype), kind="ExternalInput").ap() for k, v in arrays.items()}
    out = nc.dram_tensor("out", (B, T, D), F32, kind="ExternalOutput").ap()
    build(nc, aps, out)
    r = run_bass_kernel_spmd(nc, [{"in_" + k: v for k, v in arrays.items()}], core_ids=[0])
    return r.results[0]["out"]
```
